# Optimizing a Trainium2 kernel written in Bass

```python
import numpy as np
import jax
import jax.numpy as jnp

def _softmax(x, axis=-1):
    return jax.nn.softmax(x, axis=axis)
def _gelu(x):
    return jax.nn.gelu(x, approximate=True)
def _silu(x):
    return jax.nn.silu(x)
def _sigmoid(x):
    return jax.nn.sigmoid(x)
def _layernorm(x, axis=-1, eps=1e-5):
    m = jnp.mean(x, axis=axis, keepdims=True)
    v = jnp.var(x, axis=axis, keepdims=True)
    return (x - m) / jnp.sqrt(v + eps)
def _scatter_add(tgt, idx, src, axis=0):
    return tgt.at[idx].add(src)
def _segment_sum(src, seg, n):
    return jax.ops.segment_sum(src, seg, n)

kernel_name = 'mk_dlrm_tower_d1_rec_788a3b'

def setup_inputs(seed: int = 0):
    np.random.seed(seed)
    _w = jnp.asarray
    def _rec_inputs():
        import jax
        import jax.numpy as jnp
        _tk = jax.random.key(seed)
        dense_ctx = jax.random.normal(jax.random.fold_in(_tk, 190), (1024, 16), jnp.float32)
        ids = jnp.stack([jax.random.randint(jax.random.fold_in(_tk, 200 + f), (1024,), 0, v, jnp.int32) for f, v in enumerate([10000, 10000, 10000, 1000, 1000])], axis=1)
        tbl_0 = 0.05 * jax.random.normal(jax.random.fold_in(_tk, 500 + 0), (10000, 1024), jnp.float32)
        tbl_1 = 0.05 * jax.random.normal(jax.random.fold_in(_tk, 500 + 1), (10000, 1024), jnp.float32)
        tbl_2 = 0.05 * jax.random.normal(jax.random.fold_in(_tk, 500 + 2), (10000, 1024), jnp.float32)
        tbl_3 = 0.05 * jax.random.normal(jax.random.fold_in(_tk, 500 + 3), (1000, 1024), jnp.float32)
        tbl_4 = 0.05 * jax.random.normal(jax.random.fold_in(_tk, 500 + 4), (1000, 1024), jnp.float32)
        _rk = jax.random.fold_in(_tk, 7)
        W_top1 = 0.0155946 * jax.random.normal(jax.random.fold_in(_tk, 801), (4112, 512), jnp.float32)
        W_top2 = 0.0441942 * jax.random.normal(jax.random.fold_in(_tk, 802), (512, 256), jnp.float32)
        W_top3 = 0.0625 * jax.random.normal(jax.random.fold_in(_tk, 803), (256, 1), jnp.float32)
        b_top1 = jnp.zeros((512,), jnp.float32)
        b_top2 = jnp.zeros((256,), jnp.float32)
        return dense_ctx, ids, tbl_0, tbl_1, tbl_2, tbl_3, tbl_4, W_top1, b_top1, W_top2, b_top2, W_top3
    dense_ctx, ids, tbl_0, tbl_1, tbl_2, tbl_3, tbl_4, W_top1, b_top1, W_top2, b_top2, W_top3 = _rec_inputs()
    def _L0_rec_setup():
        import jax, jax.numpy as jnp
        import numpy as np
        B, D, H, T, NTE, NSE = (4096, 1024, 1024, 4, 2, 2)
        E = T * NTE + NSE
        K = NTE + NSE
        EXPERT_IN_IDX = np.minimum(np.arange(E) // NTE, T)
        SEL = np.array([[t * NTE + j for j in range(NTE)] + list(range(E - NSE, E)) for t in range(T)])

        def _ple_layer(x, W, b, Gw, Gb, Gsw=None, Gsb=None):
            xe = x[:, EXPERT_IN_IDX, :]
            eo = jax.nn.relu(jnp.einsum('bed,edh->beh', xe, W) + b)
            gates = jax.nn.softmax(jnp.einsum('btd,tdk->btk', x[:, :T, :], Gw) + Gb, axis=-1)
            sel_eo = eo[:, SEL, :]
            task_out = jnp.einsum('btk,btkh->bth', gates, sel_eo)
            if Gsw is None:
                return task_out
            gs = jax.nn.softmax(x[:, T, :] @ Gsw + Gsb, axis=-1)
            shared_out = jnp.einsum('be,beh->bh', gs, eo)
            return jnp.concatenate([task_out, shared_out[:, None, :]], axis=1)
        key = jax.random.key(seed)
        ks = jax.random.split(key, 8)
        s = 0.02
        return {'inputs': jax.random.normal(ks[0], (B, T + 1, D), jnp.float32), 'W0': jax.random.normal(ks[1], (E, D, H), jnp.float32) * s, 'b0': jnp.zeros((E, H), jnp.float32), 'G0w': jax.random.normal(ks[2], (T, D, K), jnp.float32) * s, 'G0b': jnp.zeros((T, K), jnp.float32), 'Gs0w': jax.random.normal(ks[3], (D, E), jnp.float32) * s, 'Gs0b': jnp.zeros((E,), jnp.float32), 'W1': jax.random.normal(ks[4], (E, H, H), jnp.float32) * s, 'b1': jnp.zeros((E, H), jnp.float32), 'G1w': jax.random.normal(ks[5], (T, H, K), jnp.float32) * s, 'G1b': jnp.zeros((T, K), jnp.float32)}
    _L0_rec_all = _L0_rec_setup()
    _L0_rec_in = {k: v for k, v in _L0_rec_all.items() if k in ('W0', 'b0', 'G0w', 'G0b', 'Gs0w', 'Gs0b', 'W1', 'b1', 'G1w', 'G1b', )}
    del _L0_rec_all

    return {
        "dense_ctx": dense_ctx,
        "ids": ids,
        "tbl_0": tbl_0,
        "tbl_1": tbl_1,
        "tbl_2": tbl_2,
        "tbl_3": tbl_3,
        "tbl_4": tbl_4,
        "W_top1": W_top1,
        "b_top1": b_top1,
        "W_top2": W_top2,
        "b_top2": b_top2,
        "W_top3": W_top3,
        "L0_rec_W0": _L0_rec_in["W0"],
        "L0_rec_b0": _L0_rec_in["b0"],
        "L0_rec_G0w": _L0_rec_in["G0w"],
        "L0_rec_G0b": _L0_rec_in["G0b"],
        "L0_rec_Gs0w": _L0_rec_in["Gs0w"],
        "L0_rec_Gs0b": _L0_rec_in["Gs0b"],
        "L0_rec_W1": _L0_rec_in["W1"],
        "L0_rec_b1": _L0_rec_in["b1"],
        "L0_rec_G1w": _L0_rec_in["G1w"],
        "L0_rec_G1b": _L0_rec_in["G1b"],
    }

def reference(dense_ctx, ids, tbl_0, tbl_1, tbl_2, tbl_3, tbl_4, W_top1, b_top1, W_top2, b_top2, W_top3, L0_rec_W0, L0_rec_b0, L0_rec_G0w, L0_rec_G0b, L0_rec_Gs0w, L0_rec_Gs0b, L0_rec_W1, L0_rec_b1, L0_rec_G1w, L0_rec_G1b):
    import jax
    import jax.numpy as jnp
    def _L0_rec_ref(inputs, W0, b0, G0w, G0b, Gs0w, Gs0b, W1, b1, G1w, G1b):
        import jax, jax.numpy as jnp
        import numpy as np
        B, D, H, T, NTE, NSE = (4096, 1024, 1024, 4, 2, 2)
        E = T * NTE + NSE
        K = NTE + NSE
        EXPERT_IN_IDX = np.minimum(np.arange(E) // NTE, T)
        SEL = np.array([[t * NTE + j for j in range(NTE)] + list(range(E - NSE, E)) for t in range(T)])

        def _ple_layer(x, W, b, Gw, Gb, Gsw=None, Gsb=None):
            xe = x[:, EXPERT_IN_IDX, :]
            eo = jax.nn.relu(jnp.einsum('bed,edh->beh', xe, W) + b)
            gates = jax.nn.softmax(jnp.einsum('btd,tdk->btk', x[:, :T, :], Gw) + Gb, axis=-1)
            sel_eo = eo[:, SEL, :]
            task_out = jnp.einsum('btk,btkh->bth', gates, sel_eo)
            if Gsw is None:
                return task_out
            gs = jax.nn.softmax(x[:, T, :] @ Gsw + Gsb, axis=-1)
            shared_out = jnp.einsum('be,beh->bh', gs, eo)
            return jnp.concatenate([task_out, shared_out[:, None, :]], axis=1)
        h = _ple_layer(inputs, W0, b0, G0w, G0b, Gs0w, Gs0b)
        return _ple_layer(h, W1, b1, G1w, G1b)

    e = jnp.stack([tbl_0[ids[:, 0]], tbl_1[ids[:, 1]], tbl_2[ids[:, 2]], tbl_3[ids[:, 3]], tbl_4[ids[:, 4]]], axis=1)
    z = _L0_rec_ref(e, L0_rec_W0, L0_rec_b0, L0_rec_G0w, L0_rec_G0b, L0_rec_Gs0w, L0_rec_Gs0b, L0_rec_W1, L0_rec_b1, L0_rec_G1w, L0_rec_G1b)
    z = z.reshape(z.shape[0], -1)
    h = jnp.concatenate([z, dense_ctx], axis=1)
    h = jnp.maximum(h @ W_top1 + b_top1, 0.0)
    h = jnp.maximum(h @ W_top2 + b_top2, 0.0)
    y = h @ W_top3
    return y


_drawn_inputs = setup_inputs


def setup_inputs(seed=0):
    import zlib

    import numpy as np

    out = dict(_drawn_inputs(seed))
    spreads = {'b_top1': (0.0, 0.1),
     'b_top2': (0.0, 0.1),
     'L0_rec_b0': (0.0, 0.1),
     'L0_rec_G0b': (0.0, 0.8),
     'L0_rec_Gs0b': (0.0, 0.8),
     'L0_rec_b1': (0.0, 0.1),
     'L0_rec_G1b': (0.0, 0.8)}
    factors = {'tbl_0': 8.0,
     'tbl_1': 8.0,
     'tbl_2': 8.0,
     'tbl_3': 8.0,
     'tbl_4': 8.0,
     'L0_rec_W0': 5.092,
     'L0_rec_G0w': 8.0,
     'L0_rec_Gs0w': 8.0,
     'L0_rec_G1w': 8.0}
    for name, (base, spread) in spreads.items():
        noise = np.random.default_rng([zlib.crc32(name.encode()), seed]).standard_normal(out[name].shape)
        drawn = base * np.exp(spread * noise) if base else spread * noise
        out[name] = jnp.asarray(drawn.astype(out[name].dtype))
    for name, factor in factors.items():
        out[name] = (out[name] * factor).astype(out[name].dtype)
    return out
```

```python
from contextlib import ExitStack

import concourse.bass as bass
from concourse import mybir

F32 = mybir.dt.float32
F32R = mybir.dt.float32r
I32 = mybir.dt.int32
ALU = mybir.AluOpType
ACT = mybir.ActivationFunctionType
AX = mybir.AxisListType

P = 128
B = 1024
D = 1024
T = 4
E = 10
KT = D // P
BT = B // P
HALF = 512
K0 = 4
KS = E
F1, F2, DC = 512, 256, 16
PAIRS = KT
UNITS = 2 * PAIRS
PASSES = 2 * T + 1
LAST = UNITS * PASSES
M1 = F1 // P
WM = 2 * P


def dlrm_tower(nc, dense_ctx, ids, tbl, W_top1, b_top1, W_top2, b_top2, W_top3,
               W0, b0, G0w, G0b, Gs0w, Gs0b, W1, b1, G1w, G1b, y):
    with ExitStack() as ctx:
        def sb(name, shape, dt=F32):
            return ctx.enter_context(nc.sbuf_tensor(name, shape, dt))

        def sem(name):
            return ctx.enter_context(nc.semaphore(name))

        eo_dram = nc.dram_tensor("eo_scratch", (2, KT, P, B), F32, kind="Internal").ap()
        part_dram = nc.dram_tensor("part_scratch", (T, KT, P, B), F32, kind="Internal").ap()
        gs_dram = nc.dram_tensor("gs_scratch", (KS, B), F32, kind="Internal").ap()
        g0_dram = nc.dram_tensor("g0_scratch", (T, K0, B), F32, kind="Internal").ap()
        g1_dram = nc.dram_tensor("g1_scratch", (T, K0, B), F32, kind="Internal").ap()

        xh = sb("xh", [P, KT, B], F32R)
        xl = sb("xl", [P, KT, B], F32R)
        A = sb("A", [P, KT, B])
        r_offset = nc.sbuf_base
        R = sb("R", [P, KT, B])
        zh = nc.alloc_sbuf_tensor_at("zh", [P, T, B], F32R, offset=r_offset)
        zl = nc.alloc_sbuf_tensor_at("zl", [P, T, B], F32R, offset=r_offset + T * B * 4)
        G = sb("G", [P, 6, B])
        eo = sb("eo", [P, 4, B])
        sp = sb("sp", [P, 2, B])
        tmp = sb("tmp", [P, B])
        ws = sb("ws", [P, 2, KT * P])
        wh = sb("wh", [P, 2, KT * P], F32R)
        wl = sb("wl", [P, 2, KT * P], F32R)
        bias = sb("bias", [P, 168])
        graw0 = sb("graw0", [P, T * KT * K0])
        graw1 = sb("graw1", [P, T * KT * K0])
        graws = sb("graws", [P, KT * KS])
        gp = sb("gp", [P, KT, 2 * KS], F32R)
        gb = sb("gb", [P, 2 * T * K0 + KS])
        ident = sb("ident", [P, P])
        idx = sb("idx", [P, BT, 5], I32)
        h1 = A[:, 0:M1, :]
        part_tile = [sp[:, 0, :], sp[:, 1, :], A[:, 6, :], A[:, 7, :]]
        g1_tiles = [G[:, 0:2, :], G[:, 2:4, :], G[:, 4:6, :], A[:, 4:6, :]]
        logit_rows = G[:, 0, :]
        soft = G[:, 1, :]
        low_part, logit, expo, prob = soft[:, 0:80], soft[:, 160:240], soft[:, 240:320], soft[:, 320:400]
        prob_rows = soft[:, 400:528]
        top, total, inverse = soft[:, 528:536], soft[:, 536:544], soft[:, 544:552]
        bias_rows = eo[:, 0, 0:2 * P]
        dense = tmp[:, 0:BT * DC].rearrange("p (b c) -> p b c", c=DC)
        h2 = eo[:, 0:2, :]
        yrow = eo[0:1, 2, :]

        pu = ctx.enter_context(nc.psum_tensor("pu", [P, 2, B], F32))
        pm = ctx.enter_context(nc.psum_tensor("pm", [P, 4, HALF], F32))
        TP_BANK = [2, 3, 0, 1]

        s_idx = sem("s_idx")
        s_rows = sem("s_rows")
        s_graw = sem("s_graw")
        s_zero = sem("s_zero")
        s_ident = sem("s_ident")
        s_btr = sem("s_btr")
        s_bias = sem("s_bias")
        w_loaded = [sem(f"w_loaded{i}") for i in range(2)]
        w_h = sem("w_h")
        w_l = sem("w_l")
        steps_done = sem("steps_done")
        relu_done = sem("relu_done")
        eo_used = sem("eo_used")
        x_free = sem("x_free")
        tp_done = sem("tp_done")
        xt_h, xt_l = sem("xt_h"), sem("xt_l")
        xs_h, xs_l = sem("xs_h"), sem("xs_l")
        gathered = [sem(f"gathered{i}") for i in range(BT)]
        gp_h, gp_l = sem("gp_h"), sem("gp_l")
        gl_done = sem("gl_done")
        gl_copied = sem("gl_copied")
        g1_done = sem("g1_done")
        soft_link = sem("soft_link")
        exp_done = sem("exp_done")
        g2_done = sem("g2_done")
        gr_copied = sem("gr_copied")
        gr_saved = sem("gr_saved")
        g_loaded = sem("g_loaded")
        gk_loaded = sem("gk_loaded")
        gs_loaded = sem("gs_loaded")
        eo_saved = [sem(f"eo_saved{i}") for i in range(4)]
        sp_loaded = sem("sp_loaded")
        sp_link = sem("sp_link")
        gate_link = sem("gate_link")
        s0_link = sem("s0_link")
        sp_used = sem("sp_used")
        h_ready = sem("h_ready")
        part_ready = sem("part_ready")
        part_saved = [sem(f"part_saved{i}") for i in range(2)]
        g1_loaded = sem("g1_loaded")
        part_loaded = [sem(f"part_loaded{i}") for i in range(T)]
        z_link = sem("z_link")
        z_used = sem("z_used")
        z_raw = sem("z_raw")
        z_h, z_l = sem("z_h"), sem("z_l")
        top_added = sem("top_added")
        s_dense = sem("s_dense")
        dense_tr = sem("dense_tr")
        dense_h, dense_l = sem("dense_h"), sem("dense_l")
        h1_relu = sem("h1_relu")
        h1_h, h1_l = sem("h1_h"), sem("h1_l")
        h2_done = sem("h2_done")
        y_done = sem("y_done")
        y_copied = sem("y_copied")
        s_out = sem("s_out")

        def pairs(eng, body):
            body(1, 1)
            with eng.Fori(0, 2) as i:
                body(2 * i + 2, 0)
                body(2 * i + 3, 1)
            body(6, 0)
            body(7, 1)

        def last_pairs(eng, body):
            body(1, 1)
            with eng.Fori(0, 3) as i:
                body(2 * i + 2, 0)
                body(2 * i + 3, 1)

        def wide(w, s, m):
            return w[:, s, :].rearrange("p (k m) -> p k m", m=m)

        w_src = [w.rearrange("e (k p) (j m) -> e j p k m", p=P, m=P) for w in (W0, W1)]
        w_top1 = W_top1[0:T * D, :].rearrange("(t j p) (c m) -> j c p t m", t=T, p=P, m=WM)
        w_top2 = W_top2.rearrange("(k p) m -> p k m", p=P)

        block = ctx.enter_context(nc.Block())

        @block.sync
        def _(sp_eng):
            sp_eng.dma_start(idx[:, :, :], ids.rearrange("(b p) f -> p b f", p=P)).then_inc(s_idx, 16)

            def load(n, s, src, dst=None):
                if not (isinstance(n, int) and n < 2):
                    sp_eng.wait_ge(w_l, n - 1)
                d = wide(ws, s, P) if dst is None else dst
                sp_eng.dma_start(d, src).then_inc(w_loaded[s], 16)

            def expert_pair(n, layer, e, j):
                load(n, 0, w_src[layer][e, j])
                load(n + 1, 1, w_src[layer][e + 1, j])

            with nc.allow_non_contiguous_dma(reason="weight tiles are rows of 512 bytes"):
                expert_pair(0, 0, 2 * T, 0)
                with sp_eng.Fori(1, PAIRS) as j:
                    expert_pair(2 * j, 0, 2 * T, j)
                with sp_eng.Fori(0, T) as t:
                    for layer in range(2):
                        with sp_eng.Fori(0, PAIRS) as j:
                            expert_pair(UNITS + 2 * UNITS * t + UNITS * layer + 2 * j, layer, 2 * t, j)
                expert_pair(LAST, 1, 2 * T, 0)
                for c in range(2):
                    load(LAST + 2 + c, c, W_top1[T * D:T * D + DC, c * WM:(c + 1) * WM], ws[0:DC, c, 0:WM])
                with sp_eng.Fori(1, PAIRS) as j:
                    expert_pair(LAST + 4 * j, 1, 2 * T, j)
                    for c in range(2):
                        load(LAST + 4 * j + 2 + c, c, w_top1[j - 1, c], wide(ws, c, WM))
                for c in range(2):
                    load(LAST + 4 * PAIRS + c, c, w_top1[PAIRS - 1, c], wide(ws, c, WM))
                load(LAST + 4 * PAIRS + 2, 0, w_top2, wide(ws, 0, WM))
            sp_eng.wait_ge(y_copied, 1)
            sp_eng.dma_start(y.rearrange("(a n) b -> a (n b)", a=1), yrow).then_inc(s_out, 16)
            sp_eng.wait_ge(s_out, 16)

        @block.gpsimd
        def _(pool):
            pool.memset(ident[:, :], 0.0).then_inc(s_zero, 1)
            pool.wait_ge(s_zero, 1)
            pool.affine_select(out=ident[:, :], in_=ident[:, :], compare_op=ALU.not_equal, fill=1.0,
                               base=0, pattern=[[-1, P]], channel_multiplier=1).then_inc(s_ident, 1)

            def gather(f):
                for b in range(BT):
                    pool.indirect_dma_start(
                        out=R[:, b, :], out_offset=None, in_=tbl[f][:, :],
                        in_offset=bass.IndirectOffsetOnAxis(ap=idx[:, b, f:f + 1], axis=0),
                    ).then_inc(gathered[b], 16)

            def save_gates(p, K, dst):
                pool.wait_ge(gr_copied, p + 1)
                pool.dma_start(dst.rearrange("k (b c) -> (k b) c", c=P), prob_rows[0:K * BT, :]).then_inc(gr_saved, 16)
                pool.wait_ge(gr_saved, 16 * (p + 1))
                if p:
                    pool.wait_ge(eo_used, PAIRS * p)

            def spread(dst, rows, done):
                pool.dma_start(dst, rows.partition_broadcast(P)).then_inc(done, 16)

            pool.wait_ge(s_idx, 16)
            gather(T)
            pool.wait_ge(xt_l, 2 * KT)
            gather(0)

            def save_eo(j, par):
                for e in range(2):
                    pool.wait_ge(relu_done, 2 * j + e + 1)
                    pool.dma_start(eo_dram[e, j], eo[:, 2 * par + e, :]).then_inc(eo_saved[2 * par + e], 16)

            save_eo(0, 0)
            save_gates(0, KS, gs_dram)
            spread(G[:, 4:6, :], gs_dram[KS - 2:KS, :], gs_loaded)
            save_eo(1, 1)
            with pool.Fori(0, 3) as i:
                save_eo(2 * i + 2, 0)
                save_eo(2 * i + 3, 1)
            for s in eo_saved:
                pool.wait_ge(s, 16 * PAIRS // 2)

            def load_eo(t, j):
                if not (isinstance(j, int) and t == j == 0):
                    pool.wait_ge(sp_used, PAIRS * t + j)
                for e in range(2):
                    pool.dma_start(sp[:, e, :], eo_dram[e, j]).then_inc(sp_loaded, 16)

            def save_part(t, j, s):
                pool.wait_ge(part_ready, PAIRS * t + j + 1)
                pool.dma_start(part_dram[t, j], sp[:, s, :]).then_inc(part_saved[s], 16)

            for t in range(T):
                load_eo(t, 0)
                pool.wait_ge(eo_used, PAIRS * max(2 * t, 1))
                spread(G[:, 4:6, :], gs_dram[2 * t:2 * t + 2, :], gs_loaded)
                save_gates(1 + 2 * t, K0, g0_dram[t])
                spread(G[:, 2:4, :], g0_dram[t, 2:4, :], gk_loaded)
                spread(G[:, 0:2, :], g0_dram[t, 0:2, :], g_loaded)
                with pool.Fori(1, PAIRS) as j:
                    load_eo(t, j)
                pool.wait_ge(xs_l, KT * (t + 1))
                if t + 1 < T:
                    gather(t + 1)
                save_gates(2 + 2 * t, K0, g1_dram[t])
                spread(G[:, 0:2, :], g1_dram[t, 0:2, :], g_loaded)
                with pool.Fori(0, PAIRS // 2) as i:
                    save_part(t, 2 * i, 0)
                    save_part(t, 2 * i + 1, 1)
                for s in part_saved:
                    pool.wait_ge(s, 16 * PAIRS // 2 * (t + 1))
            pool.wait_ge(eo_used, PAIRS * PASSES)
            pool.wait_ge(xs_l, KT * (T + 1))
            pool.wait_ge(part_ready, PAIRS * T)
            pool.dma_start(dense, dense_ctx.rearrange("(b p) c -> p b c", p=P)).then_inc(s_dense, 16)
            for t in range(T):
                spread(g1_tiles[t], g1_dram[t, 2:K0, :], g1_loaded)
            for t in range(T):
                pool.dma_start(part_tile[t], part_dram[t, 0]).then_inc(part_loaded[t], 16)
            with pool.Fori(1, PAIRS) as j:
                for t in range(T):
                    pool.wait_ge(z_l, T * (j - 1) + t + 1)
                    pool.dma_start(part_tile[t], part_dram[t, j]).then_inc(part_loaded[t], 16)

        @block.scalar
        def _(act):
            rows = [(b0.rearrange("e (j p) -> (e j) p", p=P), 0, 0, E * KT),
                    (b1.rearrange("e (j p) -> (e j) p", p=P), 1, 0, E * KT),
                    (b_top1.rearrange("(j p) -> j p", p=P), 1, 80, F1 // P),
                    (b_top2.rearrange("(j p) -> j p", p=P), 1, 84, F2 // P),
                    (W_top3.rearrange("(j p) o -> j (p o)", p=P), 1, 86, F2 // P)]
            for src, c, r, n in rows:
                act.dma_start(bias_rows[r:r + n, c * P:(c + 1) * P], src).then_inc(s_rows, 16)
            with nc.allow_non_contiguous_dma(reason="gate weights have rows of a few values"):
                act.dma_start(graws[:, :].rearrange("p (k c) -> p k c", c=KS),
                              Gs0w.rearrange("(k p) c -> p k c", p=P)).then_inc(s_graw, 16)
                for raw, w in ((graw0, G0w), (graw1, G1w)):
                    act.dma_start(raw[:, :].rearrange("p (t k c) -> p t k c", t=T, c=K0),
                                  w.rearrange("t (k p) c -> p t k c", p=P)).then_inc(s_graw, 16)
            flat = [G0b.rearrange("t k -> (t k)"), G1b.rearrange("t k -> (t k)"), Gs0b]
            at = 0
            for f in flat:
                act.dma_start(gb[:, at:at + f.shape[0]], f.partition_broadcast(P)).then_inc(s_graw, 16)
                at += f.shape[0]

            def w_high(n, s, count, free, k=slice(0, P), cols=slice(0, KT * P)):
                act.wait_ge(w_loaded[s], 16 * count)
                if free is not None:
                    act.wait_ge(steps_done, free)
                act.activation(wh[k, s, cols], ws[k, s, cols], ACT.Copy).then_inc(w_h, 1)

            def relu(m, s, slot, step, col):
                act.wait_ge(steps_done, step + 1)
                act.activation(eo[:, slot, :], pu[:, s, :], ACT.Relu, bias=bias[:, col]).then_inc(relu_done, 1)

            def gate_weights(p, raw, K):
                if not (isinstance(p, int) and p == 0):
                    act.wait_ge(gl_done, p)
                act.activation(gp[:, :, 0:K], raw.rearrange("p (k c) -> p k c", c=K), ACT.Copy).then_inc(gp_h, 1)

            def x_transposed(r, i, free):
                act.wait_ge(tp_done, 2 * KT * r + i + 1)
                if free is not None and i % 2 == 0:
                    act.wait_ge(*free(i // 2))
                act.activation(xh[:, i // 2, (i % 2) * HALF:(i % 2 + 1) * HALF], pm[:, TP_BANK[i % 4], :],
                               ACT.Copy).then_inc(xt_h, 1)

            def x_tile(src, k, ready, free):
                act.wait_ge(*ready(k))
                act.wait_ge(*free(k))
                act.activation(xh[:, k, :], src[:, k, :], ACT.Copy).then_inc(xs_h, 1)

            def freed(p):
                return lambda k: (x_free, 7 * p + k + 1) if k < 7 else (steps_done, UNITS * (p + 1))

            def one_pass(p, col, K, raw_next, K_next, x_next):
                n0, q0 = UNITS * p, PAIRS * p
                count0 = PAIRS * p

                def unit(j, e, par):
                    n = n0 + 2 * j + e
                    w_high(n + 2, e, count0 + j + 2, n + 1)
                    if e == 0:
                        if not (isinstance(p, int) and p == 0 and j < 2):
                            act.wait_ge(eo_used, q0 + j - 1)
                    if isinstance(p, int) and p == 0:
                        if not (isinstance(j, int) and j < 2):
                            act.wait_ge(eo_saved[2 * par + e], 16 * saved(j, par))
                    elif isinstance(j, int) and j < 2:
                        act.wait_ge(eo_saved[2 * par + e], 16 * PAIRS // 2)
                    relu(n, e, 2 * par + e, n, col(j, e))

                def saved(j, par):
                    if isinstance(j, int):
                        return j // 2
                    return loop_i[0] + 1

                loop_i = [None]
                act.wait_ge(gl_done, p + 1)
                if not (isinstance(p, int) and p == 0):
                    act.wait_ge(eo_used, q0)
                act.activation(logit_rows[0:2 * K, :].rearrange("k (h c) -> k h c", h=2), pm[0:2 * K, 2:4, :],
                               ACT.Copy).then_inc(gl_copied, 1)
                unit(0, 0, 0)
                act.wait_ge(soft_link, 8 * p + 5)
                act.activation(expo[:, 0:K * BT], logit[:, 0:K * BT], ACT.Exp).then_inc(exp_done, 1)
                act.wait_ge(g2_done, p + 1)
                act.activation(prob_rows[0:K * BT, :], pm[0:K * BT, 3, 0:P], ACT.Copy).then_inc(gr_copied, 1)
                unit(0, 1, 0)
                for e in range(2):
                    unit(1, e, 1)
                with act.Fori(0, 2) as i:
                    loop_i[0] = i
                    for j, par in ((2 * i + 2, 0), (2 * i + 3, 1)):
                        for e in range(2):
                            unit(j, e, par)
                for e in range(2):
                    unit(6, e, 0)
                unit(7, 0, 1)
                if raw_next is not None:
                    gate_weights(p + 1, raw_next, K_next)
                x_next(lambda: unit(7, 1, 1))

            def next_transposed(r, p):
                def go(last_unit):
                    for i in range(2 * KT):
                        x_transposed(r, i, freed(p))
                    last_unit()
                return go

            def next_sbuf(src, p, ready):
                def go(last_unit):
                    for k in range(KT - 1):
                        x_tile(src, k, ready, freed(p))
                    last_unit()
                    x_tile(src, KT - 1, ready, freed(p))
                return go

            def graw(raw, t):
                return raw[:, bass.ds(t * (KT * K0), KT * K0)]

            w_high(0, 0, 1, None)
            w_high(1, 1, 1, None)
            for i in range(2 * KT):
                x_transposed(0, i, None)
            act.wait_ge(s_graw, 16 * 6)
            gate_weights(0, graws[:, :], KS)
            act.wait_ge(s_bias, 2)

            one_pass(0, lambda j, e: bass.ds((2 * T + e) * KT + j, 1), KS, graw(graw0, 0), K0, next_transposed(1, 0))

            def task(t, nxt):
                c = 2 * KT * t
                p = 2 * t + 1
                one_pass(p, lambda j, e: bass.ds(c + e * KT + j, 1), K0, graw(graw1, t), K0,
                         next_sbuf(R, p, lambda k: (h_ready, KT * t + k + 1)))
                one_pass(p + 1, lambda j, e: bass.ds(c + (E + e) * KT + j, 1), K0, *nxt)

            with act.Fori(0, T - 1) as t:
                task(t, (graw(graw0, t + 1), K0, next_transposed(t + 2, 2 * t + 2)))
            task(T - 1, (None, None, next_sbuf(A, 2 * T, lambda k: (eo_used, PAIRS * 2 * T))))

            def last_unit(j, e, par, steps_base, units_base):
                m = LAST + 2 * j + e
                if e == 0 and isinstance(j, int) and j == 0:
                    act.wait_ge(eo_used, PAIRS * PASSES - 1)
                elif e == 0:
                    act.wait_ge(eo_used, PAIRS * PASSES)
                    if not isinstance(j, int):
                        act.wait_ge(z_used, T * (j - 1))
                relu(m, e, 2 * par + e, steps_base + e, bass.ds((E + 2 * T + e) * KT + j, 1))

            def last_pair(j, par):
                s, c0 = LAST + 6 * j, LAST // 2 + 2 * j
                first = isinstance(j, int) and j == 0
                dims = dict(k=slice(0, DC), cols=slice(0, WM)) if first else {}
                for e in range(2):
                    w_high(LAST + 4 * j + 2 + e, e, c0 + 2, s + 1 + e, **dims)
                    last_unit(j, e, par, s, LAST + 4 * j)
                if first:
                    act.wait_ge(dense_tr, 1)
                    act.wait_ge(xs_l, KT * T)
                    act.activation(zh[0:DC, 0, :].rearrange("p (h c) -> p h c", h=2), pm[0:DC, 0:2, :],
                                   ACT.Copy).then_inc(dense_h, 1)
                for e in range(2):
                    w_high(LAST + 4 * j + 4 + e, e, c0 + 3, s + 4 + 2 * e)
                for t in range(T):
                    act.wait_ge(z_raw, T * j + t + 1)
                    act.activation(zh[:, t, :], part_tile[t], ACT.Copy).then_inc(z_h, 1)

            last_pair(0, 0)
            last_pairs(act, last_pair)
            w_high(LAST + 4 * PAIRS + 2, 0, LAST // 2 + 2 * PAIRS + 2, LAST + 6 * PAIRS + 2)
            for m in range(M1):
                act.wait_ge(top_added, 4 * PAIRS + m + 1)
                act.activation(h1[:, m, :], h1[:, m, :], ACT.Relu, bias=bias[:, 160 + m:161 + m]).then_inc(h1_relu, 1)
                act.wait_ge(h1_relu, m + 1)
                act.activation(xh[:, m, :], h1[:, m, :], ACT.Copy).then_inc(h1_h, 1)
            for m in range(2):
                act.wait_ge(steps_done, LAST + 6 * PAIRS + 4 + m + 1)
                act.activation(h2[:, m, :], pu[:, m, :], ACT.Relu, bias=bias[:, 164 + m:165 + m]).then_inc(h2_done, 1)
            act.wait_ge(y_done, 1)
            act.activation(yrow.rearrange("p (h c) -> p h c", h=2), pm[0:1, 0:2, :], ACT.Copy).then_inc(y_copied, 1)

        @block.tensor
        def _(pe):
            PARTS = ((wh, xh), (wh, xl), (wl, xh))

            def product(out, w, x, start, stop):
                parts = ((w[0], x[0]), (w[0], x[1]), (w[1], x[0]))
                for i, (a, b) in enumerate(parts):
                    for h in range(2):
                        mm = pe.matmul(out[:, h * HALF:(h + 1) * HALF], a, b[:, h * HALF:(h + 1) * HALF],
                                       start=start and i == 0, stop=stop and i == 2)
                return mm

            def unit(s, before=None, after=None):
                w = wide(wh, s, P), wide(wl, s, P)
                for k in range(KT):
                    if before:
                        before(k)
                    mm = product(pu[:, s, :], (w[0][:, k, :], w[1][:, k, :]), (xh[:, k, :], xl[:, k, :]),
                                 k == 0, k == KT - 1)
                    if k == KT - 1:
                        mm.then_inc(steps_done, 1)
                    if after:
                        after(k, mm)

            def begin(n):
                pe.wait_ge(w_l, n + 1)
                if not (isinstance(n, int) and n < 2):
                    pe.wait_ge(relu_done, n - 1)

            def transpose_x(r, i):
                if not (isinstance(r, int) and r == 0 and i < 4):
                    pe.wait_ge(xt_l, 2 * KT * r + i - 3)
                k, h = divmod(i, 2)
                if k == 0:
                    for b in range(4 * h, 4 * h + 4):
                        pe.wait_ge(gathered[b], 16 * (r + 1))
                for b in range(4):
                    tr = pe.transpose(pm[:, TP_BANK[i % 4], b * P:(b + 1) * P],
                                      R[:, 4 * h + b, k * P:(k + 1) * P], ident[:, :])
                tr.then_inc(tp_done, 1)

            def one_pass(p, K, x_ready, tr_next):
                n0 = UNITS * p

                def gate_logits(k, _):
                    if k == 0:
                        pe.wait_ge(gp_l, p + 1)
                        pe.wait_ge(xt_l, x_out)
                        if not (isinstance(p, int) and p == 0):
                            pe.wait_ge(gr_copied, p)
                    for x in (xh, xl):
                        for h in range(2):
                            mm = pe.matmul(pm[0:2 * K, 2 + h, :], gp[:, k, 0:2 * K], x[:, k, h * HALF:(h + 1) * HALF],
                                           start=k == 0 and x is xh, stop=k == KT - 1 and x is xl)
                    if k == KT - 1:
                        mm.then_inc(gl_done, 1)

                def logits_by_batch(k, _):
                    if k == 0:
                        pe.wait_ge(s_ident, 1)
                        pe.wait_ge(gl_copied, p + 1)
                        for b in range(BT):
                            tr = pe.transpose(pm[:, 2, b * 2 * K:(b + 1) * 2 * K],
                                              logit_rows[0:2 * K, b * P:(b + 1) * P], ident[0:2 * K, 0:2 * K])
                        tr.then_inc(g1_done, 1)
                    if k == 4:
                        pe.wait_ge(soft_link, 8 * p + 8)
                        pe.transpose(pm[0:K * BT, 3, 0:P], prob[:, 0:K * BT], ident[:, :]).then_inc(g2_done, 1)

                def x_read(k, mm):
                    if k < KT - 1:
                        mm.then_inc(x_free, 1)
                    if tr_next is not None:
                        transpose_x(tr_next, 2 * k)
                        transpose_x(tr_next, 2 * k + 1)

                x_out = x_ready(KT)
                begin(n0)
                if isinstance(p, int) and p == 0:
                    def x_made(k):
                        if k < KT - 1:
                            transpose_x(0, 2 * k + 2)
                            transpose_x(0, 2 * k + 3)
                        pe.wait_ge(*x_ready(k))

                    unit(0, before=x_made)
                    for k in range(KT):
                        gate_logits(k, None)
                else:
                    unit(0, before=lambda k: pe.wait_ge(*x_ready(k)), after=gate_logits)
                begin(n0 + 1)
                unit(1, after=logits_by_batch)
                with pe.Fori(1, PAIRS - 1) as j:
                    for e in range(2):
                        begin(n0 + 2 * j + e)
                        unit(e)
                begin(n0 + UNITS - 2)
                unit(0)
                begin(n0 + UNITS - 1)
                unit(1, after=x_read)

            def x_from_psum(r):
                return lambda k: (xt_l, 2 * KT * r + 2 * k + 2) if k < KT else 2 * KT * r + 2 * KT - 2

            def x_from_sbuf(i, r):
                return lambda k: (xs_l, KT * i + k + 1) if k < KT else 2 * KT * r + 2 * KT

            pe.wait_ge(s_ident, 1)
            pe.wait_ge(s_rows, 16 * 5)
            for c, n in ((0, 80), (1, 88)):
                pe.transpose(pu[:, 0, c * HALF:c * HALF + n], bias_rows[0:n, c * P:(c + 1) * P],
                             ident[0:n, 0:n]).then_inc(s_btr, 1)
            for i in range(2):
                transpose_x(0, i)
            pe.wait_ge(s_bias, 2)
            one_pass(0, KS, x_from_psum(0), 1)

            def task(t, nxt):
                one_pass(2 * t + 1, K0, x_from_psum(t + 1), None)
                one_pass(2 * t + 2, K0, x_from_sbuf(t, t + 1), nxt)

            with pe.Fori(0, T - 1) as t:
                task(t, t + 2)
            task(T - 1, None)

            def top_step(j, c, m, first=False):
                rows = DC if first else P
                w = [wide(x, c, WM) for x in (wh, wl)]
                for t in range(1 if first else T):
                    if c == 0 and m == 0:
                        if first:
                            pe.wait_ge(dense_l, 1)
                        else:
                            pe.wait_ge(z_l, T * (j - 1) + t + 1)
                    mm = product(pu[:, m, :], [x[0:rows, t, m * P:(m + 1) * P] for x in w],
                                 (zh[0:rows, t, :], zl[0:rows, t, :]), t == 0, first or t == T - 1)
                mm.then_inc(steps_done, 1)

            def top(j, first=False):
                for c in range(2):
                    pe.wait_ge(w_l, LAST + 4 * j + 2 + c + 1)
                    for m in range(2):
                        if c == 0:
                            pe.wait_ge(relu_done, LAST + 2 * j + m + 1)
                        else:
                            pe.wait_ge(top_added, 4 * j + m + 1)
                        top_step(j, c, m, first)

            for e in range(2):
                begin(LAST + e)
                unit(e, before=(lambda k: pe.wait_ge(xs_l, KT * T + k + 1)) if e == 0 else None)
            pe.wait_ge(s_dense, 16)
            for b in range(BT):
                tr = pe.transpose(pm[0:DC, b // 4, (b % 4) * P:(b % 4 + 1) * P], dense[:, b, :], ident[:, :])
            tr.then_inc(dense_tr, 1)
            top(0, first=True)
            with pe.Fori(1, PAIRS) as j:
                for e in range(2):
                    pe.wait_ge(w_l, LAST + 4 * j + e + 1)
                    pe.wait_ge(top_added, 4 * (j - 1) + 3 + e)
                    unit(e)
                top(j)
            for c in range(2):
                pe.wait_ge(w_l, LAST + 4 * PAIRS + c + 1)
                for m in range(2):
                    pe.wait_ge(top_added, 4 * (PAIRS - 1) + 3 + 2 * c + m)
                    top_step(PAIRS, c, m)
            pe.wait_ge(w_l, LAST + 4 * PAIRS + 3)
            w = [wide(x, 0, WM) for x in (wh, wl)]
            for m in range(2):
                pe.wait_ge(top_added, 4 * PAIRS + 3 + m)
                for k in range(M1):
                    if m == 0:
                        pe.wait_ge(h1_l, k + 1)
                    mm = product(pu[:, m, :], [x[:, k, m * P:(m + 1) * P] for x in w],
                                 (xh[:, k, :], xl[:, k, :]), k == 0, k == M1 - 1)
                mm.then_inc(steps_done, 1)
            for k in range(2):
                pe.wait_ge(h2_done, k + 1)
                for h in range(2):
                    mm = pe.matmul(pm[0:1, h, :], bias[:, 166 + k:167 + k], h2[:, k, h * HALF:(h + 1) * HALF],
                                   start=k == 0, stop=k == 1)
            mm.then_inc(y_done, 1)

        @block.vector
        def _(dve):
            def low(out, src, high, done):
                dve.tensor_tensor(out, src, high.bitcast(F32), ALU.subtract).then_inc(done, 1)

            def w_low(n, s, k=slice(0, P), cols=slice(0, KT * P)):
                dve.wait_ge(w_h, n + 1)
                low(wl[k, s, cols], ws[k, s, cols], wh[k, s, cols], w_l)

            def gate_weights(p, raw, K):
                dve.wait_ge(gp_h, p + 1)
                low(gp[:, :, K:2 * K], raw.rearrange("p (k c) -> p k c", c=K), gp[:, :, 0:K], gp_l)

            def x_transposed(r, i):
                dve.wait_ge(xt_h, 2 * KT * r + i + 1)
                cols = slice((i % 2) * HALF, (i % 2 + 1) * HALF)
                low(xl[:, i // 2, cols], pm[:, TP_BANK[i % 4], :], xh[:, i // 2, cols], xt_l)

            def x_tile(src, r, k):
                dve.wait_ge(xs_h, KT * r + k + 1)
                low(xl[:, k, :], src[:, k, :], xh[:, k, :], xs_l)

            class Links:

                def __init__(self, s, base):
                    self.s, self.n = s, base

                def add(self, ins):
                    ins.then_inc(self.s, 1)
                    self.n = self.n + 1
                    return self.n

                def wait(self, n):
                    dve.wait_ge(self.s, n)

            def softmax(p, K, b_gates):
                N = K * BT
                L = Links(soft_link, 8 * p)
                v = lambda a: a[:, 0:N].rearrange("p (k b) -> p k b", b=BT)
                by_b = pm[:, 2, 0:2 * N].rearrange("p (b k) -> p k b", b=BT)
                dve.wait_ge(g1_done, p + 1)
                if not (isinstance(p, int) and p == 0):
                    dve.wait_ge(eo_used, PAIRS * p)
                L.wait(L.add(dve.tensor_copy(v(low_part), by_b[:, K:2 * K, :])))
                L.wait(L.add(dve.tensor_tensor(v(logit), by_b[:, 0:K, :], v(low_part), ALU.add)))
                L.wait(L.add(dve.tensor_tensor(v(logit), v(logit), b_gates.unsqueeze(2).to_broadcast([P, K, BT]),
                                               ALU.add)))
                L.wait(L.add(dve.tensor_reduce(top, v(logit).rearrange("p k b -> p b k"), AX.X, ALU.max)))
                L.wait(L.add(dve.tensor_tensor(v(logit), v(logit), top.unsqueeze(1).to_broadcast([P, K, BT]),
                                               ALU.subtract)))
                dve.wait_ge(exp_done, p + 1)
                L.wait(L.add(dve.tensor_reduce(total, v(expo).rearrange("p k b -> p b k"), AX.X, ALU.add)))
                L.wait(L.add(dve.reciprocal(inverse, total)))
                L.add(dve.tensor_tensor(v(prob), v(expo), inverse.unsqueeze(1).to_broadcast([P, K, BT]), ALU.mult))

            def one_pass(p, K, b_gates, body, after):
                n0 = UNITS * p
                w_low(n0 + 1, 1)
                w_low(n0 + 2, 0)
                softmax(p, K, b_gates)

                def pair(j, par):
                    w_low(n0 + 2 * j + 1, 1)
                    body(j - 1, 1 - par, lambda: w_low(n0 + 2 * j + 2, 0))

                pairs(dve, pair)
                after()

            def shared0(j, par, weights=lambda: None):
                L = Links(s0_link, 2 * j)
                if not (isinstance(j, int) and j == 0):
                    dve.wait_ge(eo_used, j)
                dve.wait_ge(gs_loaded, 16)
                dve.wait_ge(relu_done, 2 * j + 2)
                a = L.add(dve.tensor_tensor(A[:, j, :], eo[:, 2 * par, :], G[:, 4, :], ALU.mult))
                b = L.add(dve.tensor_tensor(tmp[:, :], eo[:, 2 * par + 1, :], G[:, 5, :], ALU.mult))
                L.wait(b)
                dve.tensor_tensor(A[:, j, :], A[:, j, :], tmp[:, :], ALU.add).then_inc(eo_used, 1)
                weights()

            def from_shared(t, j):
                L = Links(sp_link, 2 * (PAIRS * t + j))
                dve.wait_ge(gk_loaded, 16 * (t + 1))
                dve.wait_ge(sp_loaded, 32 * (PAIRS * t + j + 1))
                L.add(dve.tensor_tensor(R[:, j, :], sp[:, 0, :], G[:, 2, :], ALU.mult))
                b = L.add(dve.tensor_tensor(sp[:, 1, :], sp[:, 1, :], G[:, 3, :], ALU.mult))
                L.wait(b)
                dve.tensor_tensor(R[:, j, :], R[:, j, :], sp[:, 1, :], ALU.add).then_inc(sp_used, 1)

            def own_first(t, j, par, L):
                dve.wait_ge(relu_done, UNITS * (2 * t + 1) + 2 * j + 1)
                dve.wait_ge(g_loaded, 16 * (2 * t + 1))
                dve.wait_ge(gs_loaded, 16 * (t + 2))
                dve.wait_ge(eo_used, PAIRS * (2 * t + 1) + j)
                a = L.add(dve.tensor_tensor(tmp[:, :], eo[:, 2 * par, :], G[:, 0, :], ALU.mult))
                L.wait(a)
                L.add(dve.tensor_tensor(eo[:, 2 * par, :], eo[:, 2 * par, :], G[:, 4, :], ALU.mult))
                dve.wait_ge(sp_used, PAIRS * t + j + 1)
                L.add(dve.tensor_tensor(R[:, j, :], R[:, j, :], tmp[:, :], ALU.add))

            def own_second(t, j, par, L):
                dve.wait_ge(relu_done, UNITS * (2 * t + 1) + 2 * j + 2)
                L.wait(L.n)
                a = L.add(dve.tensor_tensor(tmp[:, :], eo[:, 2 * par + 1, :], G[:, 1, :], ALU.mult))
                L.wait(a)
                dve.tensor_tensor(R[:, j, :], R[:, j, :], tmp[:, :], ALU.add).then_inc(h_ready, 1)
                L.add(dve.tensor_tensor(eo[:, 2 * par + 1, :], eo[:, 2 * par + 1, :], G[:, 5, :], ALU.mult))

            def to_shared(t, j, par, L):
                L.add(dve.tensor_tensor(A[:, j, :], A[:, j, :], eo[:, 2 * par, :], ALU.add))
                L.wait(L.n)
                dve.tensor_tensor(A[:, j, :], A[:, j, :], eo[:, 2 * par + 1, :], ALU.add).then_inc(eo_used, 1)

            def task0(t):
                def body(j, par, weights):
                    L = Links(gate_link, 6 * (PAIRS * t + j))
                    if isinstance(j, int) and j == 0:
                        from_shared(t, j)
                    own_first(t, j, par, L)
                    own_second(t, j, par, L)
                    if isinstance(j, int) and j == 0:
                        weights()
                    to_shared(t, j, par, L)
                    if not (isinstance(j, int) and j == 0):
                        weights()
                    from_shared(t, j + 1)
                return body

            def task0_end(t):
                j, par = PAIRS - 1, 1

                def go():
                    L = Links(gate_link, 6 * (PAIRS * t + j))
                    gate_weights(2 * t + 2, raw(graw1, t), K0)
                    for k in range(4):
                        x_tile(R, t, k)
                    own_first(t, j, par, L)
                    for k in range(4, KT - 1):
                        x_tile(R, t, k)
                    own_second(t, j, par, L)
                    x_tile(R, t, KT - 1)
                    to_shared(t, j, par, L)
                return go

            def task1(t):
                def body(j, par, weights=lambda: None):
                    dve.wait_ge(g_loaded, 16 * (2 * t + 2))
                    dve.wait_ge(relu_done, UNITS * (2 * t + 2) + 2 * j + 2)
                    dve.wait_ge(eo_used, PAIRS * (2 * t + 2) + j)
                    if not (isinstance(j, int) and j == 0):
                        dve.wait_ge(part_ready, PAIRS * t + j)
                    if not (isinstance(j, int) and j < 2):
                        dve.wait_ge(part_saved[par], 16 * (PAIRS // 2) * t + 8 * (j - par))
                    dve.tensor_tensor(sp[:, par, :], eo[:, 2 * par, :], G[:, 0, :], ALU.mult)
                    dve.tensor_tensor(tmp[:, :], eo[:, 2 * par + 1, :], G[:, 1, :], ALU.mult).then_inc(eo_used, 1)
                    dve.wait_ge(eo_used, PAIRS * (2 * t + 2) + j + 1)
                    dve.tensor_tensor(sp[:, par, :], sp[:, par, :], tmp[:, :], ALU.add).then_inc(part_ready, 1)
                    weights()
                return body

            def raw(g, t):
                return g[:, bass.ds(t * (KT * K0), KT * K0)]

            for c, n in ((0, 80), (1, 88)):
                dve.wait_ge(s_btr, c + 1)
                dve.tensor_copy(bias[:, c * 80:c * 80 + n], pu[:, 0, c * HALF:c * HALF + n]).then_inc(s_bias, 1)
            w_low(0, 0)
            for i in range(2 * KT):
                x_transposed(0, i)
            dve.wait_ge(s_graw, 16 * 6)
            gate_weights(0, graws[:, :], KS)

            def shared0_end():
                gate_weights(1, raw(graw0, 0), K0)
                for i in range(2 * KT):
                    x_transposed(1, i)
                shared0(PAIRS - 1, 1)

            one_pass(0, KS, gb[:, 2 * T * K0:2 * T * K0 + KS], shared0, shared0_end)

            def task(t, last):
                one_pass(2 * t + 1, K0, gb[:, bass.ds(t * K0, K0)], task0(t), task0_end(t))

                def task1_end():
                    if last:
                        for k in range(KT):
                            x_tile(A, T, k)
                    else:
                        gate_weights(2 * t + 3, raw(graw0, t + 1), K0)
                        for i in range(2 * KT):
                            x_transposed(t + 2, i)
                    task1(t)(PAIRS - 1, 1)

                one_pass(2 * t + 2, K0, gb[:, bass.ds((T + t) * K0, K0)], task1(t), task1_end)

            with dve.Fori(0, T - 1) as t:
                task(t, False)
            task(T - 1, True)

            w_low(LAST + 1, 1)

            def z_first(j, par, t):
                L = Links(z_link, 2 * (T * j + t))
                if t:
                    L.wait(L.n)
                elif isinstance(j, int) and j == 0:
                    dve.wait_ge(part_ready, PAIRS * T)
                    dve.wait_ge(g1_loaded, 16 * T)
                else:
                    dve.wait_ge(z_raw, T * j)
                dve.wait_ge(relu_done, LAST + 2 * j + 1)
                dve.wait_ge(part_loaded[t], 16 * (j + 1))
                L.wait(L.add(dve.tensor_tensor(tmp[:, :], eo[:, 2 * par, :], g1_tiles[t][:, 0, :], ALU.mult)))
                L.add(dve.tensor_tensor(part_tile[t], part_tile[t], tmp[:, :], ALU.add))

            def z_second(j, par, t):
                dve.wait_ge(relu_done, LAST + 2 * j + 2)
                if t:
                    dve.wait_ge(z_raw, T * j + t)
                else:
                    dve.wait_ge(z_link, 2 * T * (j + 1))
                dve.tensor_tensor(tmp[:, :], eo[:, 2 * par + 1, :], g1_tiles[t][:, 1, :], ALU.mult).then_inc(z_used, 1)
                dve.wait_ge(z_used, T * j + t + 1)
                dve.tensor_tensor(part_tile[t], part_tile[t], tmp[:, :], ALU.add).then_inc(z_raw, 1)

            def add_top(j, m):
                dve.wait_ge(steps_done, LAST + 6 * j + 2 + m + 1)
                if isinstance(j, int) and j == 0:
                    dve.wait_ge(xs_l, KT * (T + 1))
                    dve.tensor_copy(h1[:, m, :], pu[:, m % 2, :]).then_inc(top_added, 1)
                else:
                    dve.wait_ge(top_added, 4 * j + m - 3)
                    dve.tensor_tensor(h1[:, m, :], pu[:, m % 2, :], h1[:, m, :], ALU.add).then_inc(top_added, 1)

            def split_z(j):
                for t in range(T):
                    dve.wait_ge(z_h, T * j + t + 1)
                    low(zl[:, t, :], part_tile[t], zh[:, t, :], z_l)

            rows = dict(k=slice(0, DC), cols=slice(0, WM))
            w_low(LAST + 2, 0, **rows)
            w_low(LAST + 3, 1, **rows)
            dve.wait_ge(dense_h, 1)
            low(zl[0:DC, 0, :].rearrange("p (h c) -> p h c", h=2), pm[0:DC, 0:2, :],
                zh[0:DC, 0, :].rearrange("p (h c) -> p h c", h=2), dense_l)
            for m in range(2):
                add_top(0, m)
            w_low(LAST + 4, 0)
            for m in range(2, M1):
                add_top(0, m)
            w_low(LAST + 5, 1)
            for t in range(T):
                z_first(0, 0, t)
            for t in range(T):
                z_second(0, 0, t)
            split_z(0)

            def last_pair(j, par):
                n = LAST + 4 * j
                w_low(n + 2, 0)
                for t in range(T):
                    z_first(j, par, t)
                w_low(n + 3, 1)
                z_second(j, par, 0)
                z_second(j, par, 1)
                add_top(j, 0)
                z_second(j, par, 2)
                add_top(j, 1)
                w_low(n + 4, 0)
                z_second(j, par, 3)
                add_top(j, 2)
                add_top(j, 3)
                w_low(n + 5, 1)
                split_z(j)

            last_pairs(dve, last_pair)
            for m in range(M1):
                dve.wait_ge(steps_done, LAST + 6 * PAIRS + m + 1)
                dve.wait_ge(top_added, 4 * (PAIRS - 1) + m + 1)
                dve.tensor_tensor(h1[:, m, :], pu[:, m % 2, :], h1[:, m, :], ALU.add).then_inc(top_added, 1)
                if m == 1:
                    w_low(LAST + 4 * PAIRS + 2, 0)
            for m in range(M1):
                dve.wait_ge(h1_h, m + 1)
                low(xl[:, m, :], h1[:, m, :], xh[:, m, :], h1_l)


_TABLES = ['tbl_0', 'tbl_1', 'tbl_2', 'tbl_3', 'tbl_4']
_FIRST = ['dense_ctx', 'ids']
_REST = ['W_top1', 'b_top1', 'W_top2', 'b_top2', 'W_top3', 'L0_rec_W0', 'L0_rec_b0', 'L0_rec_G0w', 'L0_rec_G0b',
         'L0_rec_Gs0w', 'L0_rec_Gs0b', 'L0_rec_W1', 'L0_rec_b1', 'L0_rec_G1w', 'L0_rec_G1b']


def kernel(**inputs):
    import numpy as _np
    import concourse.bacc as _bacc
    from concourse import mybir as _mybir
    from concourse.bass_utils import run_bass_kernel_spmd as _run

    nc = _bacc.Bacc("TRN2", target_bir_lowering=False, num_devices=1)
    arrays, args = {}, {}
    for name in _FIRST + _TABLES + _REST:
        a = _np.ascontiguousarray(inputs[name])
        arrays[f"in_{name}"] = a
        args[name] = nc.dram_tensor(f"in_{name}", a.shape, _mybir.dt.from_np(a.dtype), kind="ExternalInput").ap()
    y = nc.dram_tensor("y", (1024, 1), _mybir.dt.float32, kind="ExternalOutput").ap()
    dlrm_tower(nc, *[args[n] for n in _FIRST], [args[n] for n in _TABLES], *[args[n] for n in _REST], y)
    r = _run(nc, [arrays], core_ids=[0])
    return r.results[0]["y"]
```

```python
from contextlib import ExitStack

import concourse.bass as bass
from concourse import mybir

F32 = mybir.dt.float32
F32R = mybir.dt.float32r
I32 = mybir.dt.int32
ALU = mybir.AluOpType
ACT = mybir.ActivationFunctionType
AX = mybir.AxisListType

P = 128
B = 1024
D = 1024
T = 4
E = 10
KT = D // P
BT = B // P
HALF = 512
K0 = 4
KS = E
F1, F2, DC = 512, 256, 16
PAIRS = KT
UNITS = 2 * PAIRS
PASSES = 2 * T + 1
LAST = UNITS * PASSES
M1 = F1 // P
WM = 2 * P


def dlrm_tower(nc, dense_ctx, ids, tbl, W_top1, b_top1, W_top2, b_top2, W_top3,
               W0, b0, G0w, G0b, Gs0w, Gs0b, W1, b1, G1w, G1b, y):
    with ExitStack() as ctx:
        def sb(name, shape, dt=F32):
            return ctx.enter_context(nc.sbuf_tensor(name, shape, dt))

        def sem(name):
            return ctx.enter_context(nc.semaphore(name))

        eo_dram = nc.dram_tensor("eo_scratch", (2, KT, P, B), F32, kind="Internal").ap()
        part_dram = nc.dram_tensor("part_scratch", (T, KT, P, B), F32, kind="Internal").ap()
        gs_dram = nc.dram_tensor("gs_scratch", (KS, B), F32, kind="Internal").ap()
        g0_dram = nc.dram_tensor("g0_scratch", (T, K0, B), F32, kind="Internal").ap()
        g1_dram = nc.dram_tensor("g1_scratch", (T, K0, B), F32, kind="Internal").ap()
        g0w_dram = nc.dram_tensor("g0w_scratch", (T, K0, D), F32, kind="Internal").ap()

        xh = sb("xh", [P, KT, B], F32R)
        xl = sb("xl", [P, KT, B], F32R)
        A = sb("A", [P, KT, B])
        r_offset = nc.sbuf_base
        R = sb("R", [P, KT, B])
        zh = nc.alloc_sbuf_tensor_at("zh", [P, T, B], F32R, offset=r_offset)
        zl = nc.alloc_sbuf_tensor_at("zl", [P, T, B], F32R, offset=r_offset + T * B * 4)
        G = sb("G", [P, 6, B])
        eo = sb("eo", [P, 4, B])
        sp = sb("sp", [P, 2, B])
        tmp = sb("tmp", [P, B])
        ws = sb("ws", [P, 2, KT * P])
        wh = sb("wh", [P, 2, KT * P], F32R)
        wl = sb("wl", [P, 2, KT * P], F32R)
        bias = sb("bias", [P, 168])
        graw1 = sb("graw1", [P, T * KT * K0])
        graws = sb("graws", [P, KT * KS])
        gp = sb("gp", [P, KT, 2 * KS], F32R)
        gb = sb("gb", [P, 2 * T * K0 + KS])
        ident = sb("ident", [P, P])
        idx = sb("idx", [P, BT, 5], I32)
        dense = sb("dense", [P, BT, DC])
        logit0 = sb("logit0", [P, K0 * BT])
        h1 = A[:, 0:M1, :]
        part_tile = [A[:, 6, :], A[:, 7, :], sp[:, 0, :], sp[:, 1, :]]
        g1_tiles = [G[:, 2:4, :], G[:, 4:6, :], A[:, 4:6, :], G[:, 0:2, :]]
        logit_rows = G[:, 0, :]
        soft = G[:, 1, :]
        low_part, logit, expo, prob = soft[:, 0:80], soft[:, 160:240], soft[:, 240:320], soft[:, 320:400]
        prob_rows = soft[:, 400:528]
        top, total, inverse = soft[:, 528:536], soft[:, 536:544], soft[:, 544:552]
        gw_first, gw_next = G[:, 0:K0, :], G[:, 2:2 + K0, :]
        bias_rows = eo[:, 0, 0:2 * P]
        g0w_raw, g0w_sorted, g0w_rows = sp[:, 0, 0:P], sp[:, 0, P:2 * P], sp[:, 0, 2 * P:3 * P]
        h2 = sp[:, 0:2, :]
        yrow = G[0:1, 0, :]

        pu = ctx.enter_context(nc.psum_tensor("pu", [P, 2, B], F32))
        pm = ctx.enter_context(nc.psum_tensor("pm", [P, 4, HALF], F32))
        TP_BANK = [2, 3, 0, 1]

        s_idx = sem("s_idx")
        s_rows = sem("s_rows")
        s_graw = sem("s_graw")
        s_graw1 = sem("s_graw1")
        s_gb = sem("s_gb")
        s_zero = sem("s_zero")
        s_ident = sem("s_ident")
        s_btr = sem("s_btr")
        s_bias = sem("s_bias")
        w_loaded = [sem(f"w_loaded{i}") for i in range(2)]
        w_h = sem("w_h")
        w_l = sem("w_l")
        steps_done = sem("steps_done")
        relu_done = sem("relu_done")
        eo_used = sem("eo_used")
        x_free = sem("x_free")
        tp_done = sem("tp_done")
        xt_h, xt_l = sem("xt_h"), sem("xt_l")
        xs_h, xs_l = sem("xs_h"), sem("xs_l")
        gathered = [sem(f"gathered{i}") for i in range(BT)]
        gp_h, gp_l = sem("gp_h"), sem("gp_l")
        gl_done = sem("gl_done")
        gl_copied = sem("gl_copied")
        s_g0w = sem("s_g0w")
        g0w_sort = sem("g0w_sort")
        g0w_tr = sem("g0w_tr")
        g0w_row = sem("g0w_row")
        g0w_saved = sem("g0w_saved")
        gw_loaded = sem("gw_loaded")
        logit_link = sem("logit_link")
        g1_done = sem("g1_done")
        soft_link = sem("soft_link")
        exp_done = sem("exp_done")
        g2_done = sem("g2_done")
        gr_copied = sem("gr_copied")
        gr_saved = sem("gr_saved")
        g_loaded = sem("g_loaded")
        gk_loaded = sem("gk_loaded")
        gs_loaded = sem("gs_loaded")
        eo_saved = [sem(f"eo_saved{i}") for i in range(4)]
        sp_loaded = sem("sp_loaded")
        sp_link = sem("sp_link")
        gate_link = sem("gate_link")
        s0_link = sem("s0_link")
        sp_used = sem("sp_used")
        h_ready = sem("h_ready")
        part_ready = sem("part_ready")
        part_saved = [sem(f"part_saved{i}") for i in range(2)]
        g1_loaded = [sem(f"g1_loaded{i}") for i in range(T)]
        part_loaded = [sem(f"part_loaded{i}") for i in range(T)]
        z_link = sem("z_link")
        z_used = sem("z_used")
        z_raw = sem("z_raw")
        z_h, z_l = sem("z_h"), sem("z_l")
        top_added = sem("top_added")
        s_dense = sem("s_dense")
        dense_tr = sem("dense_tr")
        dense_h, dense_l = sem("dense_h"), sem("dense_l")
        h1_relu = sem("h1_relu")
        h1_h, h1_l = sem("h1_h"), sem("h1_l")
        h2_done = sem("h2_done")
        y_done = sem("y_done")
        y_copied = sem("y_copied")
        s_out = sem("s_out")

        def pairs(eng, body):
            body(1, 1)
            with eng.Fori(0, 2) as i:
                body(2 * i + 2, 0)
                body(2 * i + 3, 1)
            body(6, 0)
            body(7, 1)

        def soft_steps(kind, t=0):
            if kind == "task0":
                return 8 + 14 * t, 3, 6
            return (0 if kind == "shared0" else 14 + 14 * t), 5, 8

        def half_tile(r, i):
            return (i % KT, i // KT) if isinstance(r, int) and r == 0 else (i // 2, i % 2)

        def wide(w, s, m):
            return w[:, s, :].rearrange("p (k m) -> p k m", m=m)

        w_src = [w.rearrange("e (k p) (j m) -> e j p k m", p=P, m=P) for w in (W0, W1)]
        w_top1 = W_top1[0:T * D, :].rearrange("(t j p) (c m) -> j c p t m", t=T, p=P, m=WM)
        w_top2 = W_top2.rearrange("(k p) m -> p k m", p=P)

        block = ctx.enter_context(nc.Block())

        @block.sync
        def _(sp_eng):
            sp_eng.dma_start(idx[:, :, :], ids.rearrange("(b p) f -> p b f", p=P)).then_inc(s_idx, 16)

            def load(n, s, src, dst=None):
                if not (isinstance(n, int) and n < 2):
                    sp_eng.wait_ge(w_l, n - 1)
                d = wide(ws, s, P) if dst is None else dst
                sp_eng.dma_start(d, src).then_inc(w_loaded[s], 16)

            def expert_pair(n, layer, e, j):
                load(n, 0, w_src[layer][e, j])
                load(n + 1, 1, w_src[layer][e + 1, j])

            with nc.allow_non_contiguous_dma(reason="weight tiles are rows of 512 bytes"):
                load(0, 0, w_src[0][2 * T, 0])
                for b in range(BT):
                    sp_eng.wait_ge(gathered[b], 16)
                load(1, 1, w_src[0][2 * T + 1, 0])
                sp_eng.dma_start(graws[:, :].rearrange("p (k c) -> p k c", c=KS),
                                 Gs0w.rearrange("(k p) c -> p k c", p=P)).then_inc(s_graw, 16)
                sp_eng.dma_start(g0w_raw.rearrange("p (t k c) -> p t k c", t=T, c=K0),
                                 G0w.rearrange("t (k p) c -> p t k c", p=P)).then_inc(s_g0w, 16)
                at = 0
                for f in (G0b.rearrange("t k -> (t k)"), G1b.rearrange("t k -> (t k)"), Gs0b):
                    sp_eng.dma_start(gb[:, at:at + f.shape[0]], f.partition_broadcast(P)).then_inc(s_gb, 16)
                    at += f.shape[0]
                sp_eng.dma_start(graw1[:, :].rearrange("p (t k c) -> p t k c", t=T, c=K0),
                                 G1w.rearrange("t (k p) c -> p t k c", p=P)).then_inc(s_graw1, 16)
                sp_eng.dma_start(dense[:, :, :], dense_ctx.rearrange("(b p) c -> p b c", p=P)).then_inc(s_dense, 16)
                with sp_eng.Fori(1, PAIRS) as j:
                    expert_pair(2 * j, 0, 2 * T, j)
                with sp_eng.Fori(0, T) as t:
                    for layer in range(2):
                        with sp_eng.Fori(0, PAIRS) as j:
                            expert_pair(UNITS + 2 * UNITS * t + UNITS * layer + 2 * j, layer, 2 * t, j)
                expert_pair(LAST, 1, 2 * T, 0)
                for c in range(2):
                    load(LAST + 2 + c, c, W_top1[T * D:T * D + DC, c * WM:(c + 1) * WM], ws[0:DC, c, 0:WM])
                with sp_eng.Fori(1, PAIRS) as j:
                    expert_pair(LAST + 4 * j, 1, 2 * T, j)
                    for c in range(2):
                        load(LAST + 4 * j + 2 + c, c, w_top1[j - 1, c], wide(ws, c, WM))
                for c in range(2):
                    load(LAST + 4 * PAIRS + c, c, w_top1[PAIRS - 1, c], wide(ws, c, WM))
                load(LAST + 4 * PAIRS + 2, 0, w_top2, wide(ws, 0, WM))
            sp_eng.wait_ge(y_copied, 1)
            sp_eng.dma_start(y.rearrange("(a n) b -> a (n b)", a=1), yrow).then_inc(s_out, 16)
            sp_eng.wait_ge(s_out, 16)

        @block.gpsimd
        def _(pool):
            pool.memset(ident[:, :], 0.0).then_inc(s_zero, 1)
            pool.wait_ge(s_zero, 1)
            pool.affine_select(out=ident[:, :], in_=ident[:, :], compare_op=ALU.not_equal, fill=1.0,
                               base=0, pattern=[[-1, P]], channel_multiplier=1).then_inc(s_ident, 1)

            def gather(f):
                for b in range(BT):
                    pool.indirect_dma_start(
                        out=R[:, b, :], out_offset=None, in_=tbl[f][:, :],
                        in_offset=bass.IndirectOffsetOnAxis(ap=idx[:, b, f:f + 1], axis=0),
                    ).then_inc(gathered[b], 16)

            def save_gates(p, K, dst):
                pool.wait_ge(gr_copied, p + 1)
                pool.dma_start(dst.rearrange("k (b c) -> (k b) c", c=P), prob_rows[0:K * BT, :]).then_inc(gr_saved, 16)
                pool.wait_ge(gr_saved, 16 * (p + 1))
                if p:
                    pool.wait_ge(eo_used, PAIRS * p)

            def spread(dst, rows, done):
                pool.dma_start(dst, rows.partition_broadcast(P)).then_inc(done, 16)

            pool.wait_ge(s_idx, 16)
            gather(T)
            pool.wait_ge(xt_l, 2 * KT)
            gather(0)

            def save_eo(j, par):
                for e in range(2):
                    pool.wait_ge(relu_done, 2 * j + e + 1)
                    pool.dma_start(eo_dram[e, j], eo[:, 2 * par + e, :]).then_inc(eo_saved[2 * par + e], 16)

            save_eo(0, 0)
            save_gates(0, KS, gs_dram)
            spread(G[:, 4:6, :], gs_dram[KS - 2:KS, :], gs_loaded)
            pool.wait_ge(g0w_row, 1)
            pool.dma_start(g0w_dram.rearrange("t c (k p) -> (t c k) p", p=P), g0w_rows).then_inc(g0w_saved, 16)
            pool.wait_ge(g0w_saved, 16)
            spread(gw_first, g0w_dram[0], gw_loaded)
            save_eo(1, 1)
            with pool.Fori(0, 3) as i:
                save_eo(2 * i + 2, 0)
                save_eo(2 * i + 3, 1)
            for s in eo_saved:
                pool.wait_ge(s, 16 * PAIRS // 2)

            def load_eo(t, j):
                if not (isinstance(j, int) and t == j == 0):
                    pool.wait_ge(sp_used, PAIRS * t + j)
                for e in range(2):
                    pool.dma_start(sp[:, e, :], eo_dram[e, j]).then_inc(sp_loaded, 16)

            def save_part(t, j, s):
                pool.wait_ge(part_ready, PAIRS * t + j + 1)
                pool.dma_start(part_dram[t, j], sp[:, s, :]).then_inc(part_saved[s], 16)

            for t in range(T):
                load_eo(t, 0)
                pool.wait_ge(eo_used, PAIRS * max(2 * t, 1))
                pool.wait_ge(logit_link, K0 * BT * (t + 1))
                spread(G[:, 4:6, :], gs_dram[2 * t:2 * t + 2, :], gs_loaded)
                save_gates(1 + 2 * t, K0, g0_dram[t])
                spread(G[:, 2:4, :], g0_dram[t, 2:4, :], gk_loaded)
                spread(G[:, 0:2, :], g0_dram[t, 0:2, :], g_loaded)
                with pool.Fori(1, PAIRS) as j:
                    load_eo(t, j)
                if t + 1 < T:
                    pool.wait_ge(xs_l, KT * (t + 1))
                    gather(t + 1)
                    pool.wait_ge(eo_used, PAIRS * (2 * t + 2))
                    spread(gw_next, g0w_dram[t + 1], gw_loaded)
                save_gates(2 + 2 * t, K0, g1_dram[t])
                spread(G[:, 0:2, :], g1_dram[t, 0:2, :], g_loaded)
                if t == T - 1:
                    for i in range(2):
                        spread(g1_tiles[i], g1_dram[i, 2:K0, :], g1_loaded[i])
                with pool.Fori(0, PAIRS // 2 - 1) as i:
                    save_part(t, 2 * i, 0)
                    save_part(t, 2 * i + 1, 1)
                save_part(t, PAIRS - 2, 0)
                if t == T - 1:
                    pool.wait_ge(xs_l, KT * (T + 1))
                    for i in range(2):
                        pool.dma_start(part_tile[i], part_dram[i, 0]).then_inc(part_loaded[i], 16)
                    spread(g1_tiles[2], g1_dram[2, 2:K0, :], g1_loaded[2])
                save_part(t, PAIRS - 1, 1)
                if t == T - 1:
                    pool.wait_ge(eo_used, PAIRS * PASSES)
                    spread(g1_tiles[3], g1_dram[3, 2:K0, :], g1_loaded[3])
                for s in part_saved:
                    pool.wait_ge(s, 16 * PAIRS // 2 * (t + 1))
            for t in range(2, T):
                pool.dma_start(part_tile[t], part_dram[t, 0]).then_inc(part_loaded[t], 16)
            with pool.Fori(1, PAIRS) as j:
                for t in range(T):
                    pool.wait_ge(z_l, T * (j - 1) + t + 1)
                    pool.dma_start(part_tile[t], part_dram[t, j]).then_inc(part_loaded[t], 16)

        @block.scalar
        def _(act):
            rows = [(b0.rearrange("e (j p) -> (e j) p", p=P), 0, 0, E * KT),
                    (b1.rearrange("e (j p) -> (e j) p", p=P), 1, 0, E * KT),
                    (b_top1.rearrange("(j p) -> j p", p=P), 1, 80, F1 // P),
                    (b_top2.rearrange("(j p) -> j p", p=P), 1, 84, F2 // P),
                    (W_top3.rearrange("(j p) o -> j (p o)", p=P), 1, 86, F2 // P)]
            for src, c, r, n in rows:
                act.dma_start(bias_rows[r:r + n, c * P:(c + 1) * P], src).then_inc(s_rows, 16)

            def w_high(n, s, count, free, k=slice(0, P), cols=slice(0, KT * P)):
                act.wait_ge(w_loaded[s], 16 * count)
                if free is not None:
                    act.wait_ge(steps_done, free)
                act.activation(wh[k, s, cols], ws[k, s, cols], ACT.Copy).then_inc(w_h, 1)

            def relu(m, s, slot, step, col):
                act.wait_ge(steps_done, step + 1)
                act.activation(eo[:, slot, :], pu[:, s, :], ACT.Relu, bias=bias[:, col]).then_inc(relu_done, 1)

            def gate_weights(g, raw, K):
                if not (isinstance(g, int) and g == 0):
                    act.wait_ge(gl_done, g)
                act.activation(gp[:, :, 0:K], raw.rearrange("p (k c) -> p k c", c=K), ACT.Copy).then_inc(gp_h, 1)

            def x_transposed(r, i, free):
                act.wait_ge(tp_done, 2 * KT * r + i + 1)
                k, h = half_tile(r, i)
                if free is not None and h == 0:
                    act.wait_ge(*free(k))
                act.activation(xh[:, k, h * HALF:(h + 1) * HALF], pm[:, TP_BANK[i % 4], :],
                               ACT.Copy).then_inc(xt_h, 1)

            def x_tile(src, k, ready, free):
                act.wait_ge(*ready(k))
                act.wait_ge(*free(k))
                act.activation(xh[:, k, :], src[:, k, :], ACT.Copy).then_inc(xs_h, 1)

            def freed(p):
                return lambda k: (x_free, 7 * p + k + 1) if k < 7 else (steps_done, UNITS * (p + 1))

            def one_pass(kind, p, g, t, col, K, weights_next, x_next):
                n0, q0 = UNITS * p, PAIRS * p
                first = isinstance(p, int) and p == 0

                def unit(j, e, par, round_=None):
                    n = n0 + 2 * j + e
                    w_high(n + 2, e, q0 + j + 2, n + 1)
                    if e == 0 and not (first and j_below(j, 2)):
                        act.wait_ge(eo_used, q0 + j - 1)
                    if first and not j_below(j, 2):
                        act.wait_ge(eo_saved[2 * par + e], 16 * (j // 2 if round_ is None else round_))
                    elif not first and j_below(j, 2):
                        act.wait_ge(eo_saved[2 * par + e], 16 * PAIRS // 2)
                    relu(n, e, 2 * par + e, n, col(j, e))

                def exps():
                    before, to_exp, _ = soft_steps(kind, t)
                    act.wait_ge(soft_link, before + to_exp)
                    act.activation(expo[:, 0:K * BT], logit[:, 0:K * BT], ACT.Exp).then_inc(exp_done, 1)

                def gates_out():
                    act.wait_ge(g2_done, p + 1)
                    act.activation(prob_rows[0:K * BT, :], pm[0:K * BT, 3, 0:P], ACT.Copy).then_inc(gr_copied, 1)

                if kind == "task0":
                    exps()
                    gates_out()
                    unit(0, 0, 0)
                else:
                    act.wait_ge(gl_done, g + 1)
                    if not first:
                        act.wait_ge(eo_used, q0)
                    act.activation(logit_rows[0:2 * K, :].rearrange("k (h c) -> k h c", h=2), pm[0:2 * K, 2:4, :],
                                   ACT.Copy).then_inc(gl_copied, 1)
                    unit(0, 0, 0)
                    exps()
                    gates_out()
                unit(0, 1, 0)
                for e in range(2):
                    unit(1, e, 1)
                with act.Fori(0, 2) as i:
                    for j, par in ((2 * i + 2, 0), (2 * i + 3, 1)):
                        for e in range(2):
                            unit(j, e, par, i + 1)
                for e in range(2):
                    unit(6, e, 0)
                unit(7, 0, 1)
                if weights_next is not None:
                    gate_weights(*weights_next)
                x_next(lambda: unit(7, 1, 1))

            def j_below(j, n):
                return isinstance(j, int) and j < n

            def next_transposed(r, p):
                def go(last_unit):
                    for i in range(2 * KT):
                        x_transposed(r, i, freed(p))
                    last_unit()
                return go

            def next_sbuf(src, p, ready):
                def go(last_unit):
                    for k in range(KT - 1):
                        x_tile(src, k, ready, freed(p))
                    last_unit()
                    x_tile(src, KT - 1, ready, freed(p))
                return go

            def graw(raw, t):
                return raw[:, bass.ds(t * (KT * K0), KT * K0)]

            w_high(0, 0, 1, None)
            for i in range(2 * KT):
                x_transposed(0, i, None)
            w_high(1, 1, 1, None)
            act.wait_ge(s_graw, 16)
            gate_weights(0, graws[:, :], KS)
            act.wait_ge(s_bias, 2)

            one_pass("shared0", 0, 0, 0, lambda j, e: bass.ds((2 * T + e) * KT + j, 1), KS, None,
                     next_transposed(1, 0))

            def task(t, x_next):
                c = 2 * KT * t
                p = 2 * t + 1
                one_pass("task0", p, None, t, lambda j, e: bass.ds(c + e * KT + j, 1), K0, (t + 1, graw(graw1, t), K0),
                         next_sbuf(R, p, lambda k: (h_ready, KT * t + k + 1)))
                one_pass("task1", p + 1, t + 1, t, lambda j, e: bass.ds(c + (E + e) * KT + j, 1), K0, None, x_next)

            act.wait_ge(s_graw1, 16)
            with act.Fori(0, T - 1) as t:
                task(t, next_transposed(t + 2, 2 * t + 2))
            task(T - 1, next_sbuf(A, 2 * T, lambda k: (eo_used, PAIRS * 2 * T)))

            def last_unit(j, e, par, step):
                if e == 0 and j_below(j, 1):
                    act.wait_ge(eo_used, PAIRS * PASSES - 1)
                elif e == 0:
                    act.wait_ge(eo_used, PAIRS * PASSES)
                    if not j_below(j, 2):
                        act.wait_ge(z_used, T * (j - 1))
                relu(LAST + 2 * j + e, e, 2 * par + e, step, bass.ds((E + 2 * T + e) * KT + j, 1))

            def last_pair(j, par):
                s, c0 = LAST + 6 * j, LAST // 2 + 2 * j
                first, last = j_below(j, 1), isinstance(j, int) and j == PAIRS - 1
                dims = dict(k=slice(0, DC), cols=slice(0, WM)) if first else {}
                for e in range(2):
                    w_high(LAST + 4 * j + 2 + e, e, c0 + 2, s + 1 + e, **dims)
                    last_unit(j, e, par, s + e)
                def next_weights(e):
                    w_high(LAST + 4 * j + 4 + e, e, c0 + 3, s + 4 + 2 * e)

                def z_high(t):
                    act.wait_ge(z_raw, T * j + t + 1)
                    act.activation((xh if last else zh)[:, t, :], part_tile[t], ACT.Copy).then_inc(z_h, 1)

                if last:
                    z_high(0)
                    z_high(1)
                    next_weights(0)
                    z_high(2)
                    z_high(3)
                    next_weights(1)
                else:
                    next_weights(0)
                    next_weights(1)
                    for t in range(T):
                        z_high(t)

            act.wait_ge(dense_tr, 1)
            act.wait_ge(xs_l, KT * T)
            act.activation(zh[0:DC, 0, :].rearrange("p (h c) -> p h c", h=2), pm[0:DC, 0:2, :],
                           ACT.Copy).then_inc(dense_h, 1)
            last_pair(0, 0)
            pairs(act, last_pair)
            w_high(LAST + 4 * PAIRS + 2, 0, LAST // 2 + 2 * PAIRS + 2, LAST + 6 * PAIRS + 2)
            for m in range(M1):
                act.wait_ge(top_added, 4 * PAIRS + m + 1)
                act.activation(zh[:, m, :], h1[:, m, :], ACT.Relu, bias=bias[:, 160 + m:161 + m]).then_inc(h1_h, 1)
            for m in range(2):
                act.wait_ge(steps_done, LAST + 6 * PAIRS + 4 + m + 1)
                act.activation(h2[:, m, :], pu[:, m, :], ACT.Relu, bias=bias[:, 164 + m:165 + m]).then_inc(h2_done, 1)
            act.wait_ge(y_done, 1)
            act.activation(yrow.rearrange("p (h c) -> p h c", h=2), pm[0:1, 0:2, :], ACT.Copy).then_inc(y_copied, 1)

        @block.tensor
        def _(pe):
            def product(out, w, x, start, stop, halves=(0, 1)):
                parts = ((w[0], x[0]), (w[0], x[1]), (w[1], x[0]))
                for i, (a, b) in enumerate(parts):
                    for h in halves:
                        mm = pe.matmul(out[:, h * HALF:(h + 1) * HALF], a, b[:, h * HALF:(h + 1) * HALF],
                                       start=start and i == 0, stop=stop and i == 2)
                return mm

            def unit(s, before=None, after=None, halves=(0, 1), last=True):
                w = wide(wh, s, P), wide(wl, s, P)
                for k in range(KT):
                    if before:
                        before(k)
                    mm = product(pu[:, s, :], (w[0][:, k, :], w[1][:, k, :]), (xh[:, k, :], xl[:, k, :]),
                                 k == 0, k == KT - 1, halves)
                    if k == KT - 1 and last:
                        mm.then_inc(steps_done, 1)
                    if after:
                        after(k, mm)

            def begin(n):
                pe.wait_ge(w_l, n + 1)
                if not (isinstance(n, int) and n < 2):
                    pe.wait_ge(relu_done, n - 1)

            def transpose_x(r, i):
                if not (isinstance(r, int) and r == 0 and i < 4):
                    pe.wait_ge(xt_l, 2 * KT * r + i - 3)
                k, h = half_tile(r, i)
                if k == 0:
                    for b in range(4 * h, 4 * h + 4):
                        pe.wait_ge(gathered[b], 16 * (r + 1))
                for b in range(4):
                    tr = pe.transpose(pm[:, TP_BANK[i % 4], b * P:(b + 1) * P],
                                      R[:, 4 * h + b, k * P:(k + 1) * P], ident[:, :])
                tr.then_inc(tp_done, 1)

            def one_pass(kind, p, g, t, K, x_ready, x_out, tr_next):
                n0 = UNITS * p
                before, _, steps = soft_steps(kind, t)

                def gate_logits(k, _=None):
                    if k == 0:
                        pe.wait_ge(gp_l, g + 1)
                        pe.wait_ge(xt_l, x_out)
                        if not (isinstance(p, int) and p == 0):
                            pe.wait_ge(gr_copied, p)
                    for x in (xh, xl):
                        for h in range(2):
                            mm = pe.matmul(pm[0:2 * K, 2 + h, :], gp[:, k, 0:2 * K], x[:, k, h * HALF:(h + 1) * HALF],
                                           start=k == 0 and x is xh, stop=k == KT - 1 and x is xl)
                    if k == KT - 1:
                        mm.then_inc(gl_done, 1)

                def logits_by_batch():
                    pe.wait_ge(s_ident, 1)
                    pe.wait_ge(gl_copied, g + 1)
                    for b in range(BT):
                        tr = pe.transpose(pm[:, 2, b * 2 * K:(b + 1) * 2 * K],
                                          logit_rows[0:2 * K, b * P:(b + 1) * P], ident[0:2 * K, 0:2 * K])
                    tr.then_inc(g1_done, 1)

                def gates_by_rows():
                    pe.wait_ge(soft_link, before + steps)
                    pe.transpose(pm[0:K * BT, 3, 0:P], prob[:, 0:K * BT], ident[:, :]).then_inc(g2_done, 1)

                def gates_in_unit(k, _):
                    if k == 0:
                        logits_by_batch()
                    if k == 4:
                        gates_by_rows()

                def gates_in_first_unit(k, _):
                    if k == KT - 1:
                        pe.wait_ge(xt_l, x_out)
                        gates_by_rows()

                def x_read(k, mm):
                    if k < KT - 1:
                        mm.then_inc(x_free, 1)
                    if tr_next is not None:
                        transpose_x(tr_next, 2 * k)
                        transpose_x(tr_next, 2 * k + 1)

                begin(n0)
                if kind == "shared0":
                    for h in range(2):
                        def x_made(k):
                            i = h * KT + k
                            if i + 2 < 2 * KT:
                                transpose_x(0, i + 2)
                            pe.wait_ge(xt_l, i + 1)

                        unit(0, before=x_made, halves=(h,), last=h == 1)
                    for k in range(KT):
                        gate_logits(k)
                    pe.wait_ge(g0w_sort, 1)
                    pe.transpose(pm[:, 0, 0:P], g0w_sorted, ident[:, :]).then_inc(g0w_tr, 1)
                else:
                    unit(0, before=lambda k: pe.wait_ge(*x_ready(k)),
                         after=gates_in_first_unit if kind == "task0" else gate_logits)
                begin(n0 + 1)
                unit(1, after=None if kind == "task0" else gates_in_unit)
                with pe.Fori(1, PAIRS - 1) as j:
                    for e in range(2):
                        begin(n0 + 2 * j + e)
                        unit(e)
                begin(n0 + UNITS - 2)
                unit(0)
                begin(n0 + UNITS - 1)
                unit(1, after=x_read)

            pe.wait_ge(s_ident, 1)
            pe.wait_ge(s_rows, 16 * 5)
            for c, n in ((0, 80), (1, 88)):
                pe.transpose(pu[:, 1, c * HALF:c * HALF + n], bias_rows[0:n, c * P:(c + 1) * P],
                             ident[0:n, 0:n]).then_inc(s_btr, 1)
            transpose_x(0, 0)
            transpose_x(0, 1)
            pe.wait_ge(s_bias, 2)
            one_pass("shared0", 0, 0, 0, KS, None, 2 * KT, 1)

            def task(t, nxt):
                r = t + 1
                one_pass("task0", 2 * t + 1, None, t, K0, lambda k: (xt_l, 2 * KT * r + 2 * k + 2), 2 * KT * r + 14,
                         None)
                one_pass("task1", 2 * t + 2, t + 1, t, K0, lambda k: (xs_l, KT * t + k + 1), 2 * KT * (r + 1), nxt)

            with pe.Fori(0, T - 1) as t:
                task(t, t + 2)
            task(T - 1, None)

            def top_step(j, c, m, first=False):
                rows = DC if first else P
                last = isinstance(j, int) and j == PAIRS
                z = (xh, xl) if last else (zh, zl)
                w = [wide(x, c, WM) for x in (wh, wl)]
                for t in range(1 if first else T):
                    if c == 0 and m == 0:
                        if first:
                            pe.wait_ge(dense_l, 1)
                        else:
                            pe.wait_ge(z_l, T * (j - 1) + t + 1)
                    mm = product(pu[:, m, :], [x[0:rows, t, m * P:(m + 1) * P] for x in w],
                                 (z[0][0:rows, t, :], z[1][0:rows, t, :]), t == 0, first or t == T - 1)
                mm.then_inc(steps_done, 1)

            def top(j, first=False):
                for c in range(2):
                    pe.wait_ge(w_l, LAST + 4 * j + 2 + c + 1)
                    for m in range(2):
                        if c == 0:
                            pe.wait_ge(relu_done, LAST + 2 * j + m + 1)
                        else:
                            pe.wait_ge(top_added, 4 * j + m + 1)
                        top_step(j, c, m, first)

            pe.wait_ge(s_dense, 16)
            for b in range(BT):
                tr = pe.transpose(pm[0:DC, b // 4, (b % 4) * P:(b % 4 + 1) * P], dense[:, b, :], ident[:, :])
            tr.then_inc(dense_tr, 1)
            for e in range(2):
                begin(LAST + e)
                unit(e, before=(lambda k: pe.wait_ge(xs_l, KT * T + k + 1)) if e == 0 else None)
            top(0, first=True)
            with pe.Fori(1, PAIRS) as j:
                for e in range(2):
                    pe.wait_ge(w_l, LAST + 4 * j + e + 1)
                    pe.wait_ge(top_added, 4 * (j - 1) + 3 + e)
                    unit(e)
                top(j)
            for c in range(2):
                pe.wait_ge(w_l, LAST + 4 * PAIRS + c + 1)
                for m in range(2):
                    pe.wait_ge(top_added, 4 * (PAIRS - 1) + 3 + 2 * c + m)
                    top_step(PAIRS, c, m)
            pe.wait_ge(w_l, LAST + 4 * PAIRS + 3)
            w = [wide(x, 0, WM) for x in (wh, wl)]
            for m in range(2):
                pe.wait_ge(top_added, 4 * PAIRS + 3 + m)
                for k in range(M1):
                    if m == 0:
                        pe.wait_ge(h1_l, k + 1)
                    mm = product(pu[:, m, :], [x[:, k, m * P:(m + 1) * P] for x in w],
                                 (zh[:, k, :], zl[:, k, :]), k == 0, k == M1 - 1)
                mm.then_inc(steps_done, 1)
            for k in range(2):
                pe.wait_ge(h2_done, k + 1)
                for h in range(2):
                    mm = pe.matmul(pm[0:1, h, :], bias[:, 166 + k:167 + k], h2[:, k, h * HALF:(h + 1) * HALF],
                                   start=k == 0, stop=k == 1)
            mm.then_inc(y_done, 1)

        @block.vector
        def _(dve):
            def low(out, src, high, done):
                dve.tensor_tensor(out, src, high.bitcast(F32), ALU.subtract).then_inc(done, 1)

            def w_low(n, s, k=slice(0, P), cols=slice(0, KT * P)):
                dve.wait_ge(w_h, n + 1)
                low(wl[k, s, cols], ws[k, s, cols], wh[k, s, cols], w_l)

            def gate_weights(g, raw, K):
                dve.wait_ge(gp_h, g + 1)
                low(gp[:, :, K:2 * K], raw.rearrange("p (k c) -> p k c", c=K), gp[:, :, 0:K], gp_l)

            def x_transposed(r, i):
                dve.wait_ge(xt_h, 2 * KT * r + i + 1)
                k, h = half_tile(r, i)
                cols = slice(h * HALF, (h + 1) * HALF)
                low(xl[:, k, cols], pm[:, TP_BANK[i % 4], :], xh[:, k, cols], xt_l)

            def x_tile(src, r, k):
                dve.wait_ge(xs_h, KT * r + k + 1)
                low(xl[:, k, :], src[:, k, :], xh[:, k, :], xs_l)

            class Links:

                def __init__(self, s, base):
                    self.s, self.n = s, base

                def add(self, ins):
                    ins.then_inc(self.s, 1)
                    self.n = self.n + 1
                    return self.n

                def wait(self, n):
                    dve.wait_ge(self.s, n)

            def softmax(kind, p, g, t, K, b_gates):
                N = K * BT
                L = Links(soft_link, soft_steps(kind, t)[0])
                v = lambda a: a[:, 0:N].rearrange("p (k b) -> p k b", b=BT)
                bias_b = b_gates.unsqueeze(2).to_broadcast([P, K, BT])
                if not (isinstance(p, int) and p == 0):
                    dve.wait_ge(eo_used, PAIRS * p)
                if kind == "task0":
                    dve.wait_ge(logit_link, K0 * BT * (t + 1))
                    L.wait(L.add(dve.tensor_tensor(v(logit), v(logit0), bias_b, ALU.add)))
                else:
                    by_b = pm[:, 2, 0:2 * N].rearrange("p (b k) -> p k b", b=BT)
                    dve.wait_ge(g1_done, g + 1)
                    L.wait(L.add(dve.tensor_copy(v(low_part), by_b[:, K:2 * K, :])))
                    L.wait(L.add(dve.tensor_tensor(v(logit), by_b[:, 0:K, :], v(low_part), ALU.add)))
                    L.wait(L.add(dve.tensor_tensor(v(logit), v(logit), bias_b, ALU.add)))
                L.wait(L.add(dve.tensor_reduce(top, v(logit).rearrange("p k b -> p b k"), AX.X, ALU.max)))
                L.wait(L.add(dve.tensor_tensor(v(logit), v(logit), top.unsqueeze(1).to_broadcast([P, K, BT]),
                                               ALU.subtract)))
                dve.wait_ge(exp_done, p + 1)
                L.wait(L.add(dve.tensor_reduce(total, v(expo).rearrange("p k b -> p b k"), AX.X, ALU.add)))
                L.wait(L.add(dve.reciprocal(inverse, total)))
                L.add(dve.tensor_tensor(v(prob), v(expo), inverse.unsqueeze(1).to_broadcast([P, K, BT]), ALU.mult))

            LOGIT_TILES = [(), (), (0,), (1,), (2, 3), (4, 5), (6, 7), ()]

            def next_logits(r, weights, tmp_free, j, tiles):
                if tiles:
                    dve.wait_ge(tmp_free[0], tmp_free[1] + j)
                for b in tiles:
                    dve.wait_ge(gathered[b], 16 * (r + 2))
                    if b == 0:
                        dve.wait_ge(gw_loaded, 16 * (r + 1))
                    for c in range(K0):
                        n = K0 * BT * r + K0 * b + c
                        if b or c:
                            dve.wait_ge(logit_link, n)
                        dve.tensor_tensor_reduce(tmp[:, :], R[:, b, :], weights[:, c, :], 1.0, 0.0, ALU.mult, ALU.add,
                                                 logit0[:, c * BT + b:c * BT + b + 1]).then_inc(logit_link, 1)

            def one_pass(kind, p, g, t, K, b_gates, body, after, logits=None):
                n0 = UNITS * p
                w_low(n0 + 1, 1)
                if kind == "task0":
                    softmax(kind, p, g, t, K, b_gates)
                    w_low(n0 + 2, 0)
                else:
                    w_low(n0 + 2, 0)
                    softmax(kind, p, g, t, K, b_gates)
                if kind == "shared0":
                    dve.wait_ge(g0w_tr, 1)
                    dve.tensor_copy(g0w_rows, pm[:, 0, 0:P]).then_inc(g0w_row, 1)

                def pair(j, par):
                    w_low(n0 + 2 * j + 1, 1)
                    body(j - 1, 1 - par, lambda: w_low(n0 + 2 * j + 2, 0))

                if logits is None:
                    pairs(dve, pair)
                else:
                    for j in range(1, PAIRS):
                        pair(j, j % 2)
                        logits(j, LOGIT_TILES[j])
                after()

            def wait_logits(r, j):
                done = sum(len(LOGIT_TILES[i]) for i in range(j + 1))
                if done:
                    dve.wait_ge(logit_link, K0 * (BT * r + done))

            def shared0(j, par, weights=lambda: None):
                L = Links(s0_link, 2 * j)
                if j:
                    dve.wait_ge(eo_used, j)
                wait_logits(0, j)
                dve.wait_ge(gs_loaded, 16)
                dve.wait_ge(relu_done, 2 * j + 2)
                L.add(dve.tensor_tensor(A[:, j, :], eo[:, 2 * par, :], G[:, 4, :], ALU.mult))
                L.wait(L.add(dve.tensor_tensor(tmp[:, :], eo[:, 2 * par + 1, :], G[:, 5, :], ALU.mult)))
                dve.tensor_tensor(A[:, j, :], A[:, j, :], tmp[:, :], ALU.add).then_inc(eo_used, 1)
                weights()

            def from_shared(t, j):
                L = Links(sp_link, 2 * (PAIRS * t + j))
                dve.wait_ge(gk_loaded, 16 * (t + 1))
                dve.wait_ge(sp_loaded, 32 * (PAIRS * t + j + 1))
                L.add(dve.tensor_tensor(R[:, j, :], sp[:, 0, :], G[:, 2, :], ALU.mult))
                L.wait(L.add(dve.tensor_tensor(sp[:, 1, :], sp[:, 1, :], G[:, 3, :], ALU.mult)))
                dve.tensor_tensor(R[:, j, :], R[:, j, :], sp[:, 1, :], ALU.add).then_inc(sp_used, 1)

            def own_first(t, j, par, L):
                dve.wait_ge(relu_done, UNITS * (2 * t + 1) + 2 * j + 1)
                dve.wait_ge(g_loaded, 16 * (2 * t + 1))
                dve.wait_ge(gs_loaded, 16 * (t + 2))
                dve.wait_ge(eo_used, PAIRS * (2 * t + 1) + j)
                L.wait(L.add(dve.tensor_tensor(tmp[:, :], eo[:, 2 * par, :], G[:, 0, :], ALU.mult)))
                L.add(dve.tensor_tensor(eo[:, 2 * par, :], eo[:, 2 * par, :], G[:, 4, :], ALU.mult))
                dve.wait_ge(sp_used, PAIRS * t + j + 1)
                L.add(dve.tensor_tensor(R[:, j, :], R[:, j, :], tmp[:, :], ALU.add))

            def own_second(t, j, par, L):
                dve.wait_ge(relu_done, UNITS * (2 * t + 1) + 2 * j + 2)
                L.wait(L.n)
                L.wait(L.add(dve.tensor_tensor(tmp[:, :], eo[:, 2 * par + 1, :], G[:, 1, :], ALU.mult)))
                dve.tensor_tensor(R[:, j, :], R[:, j, :], tmp[:, :], ALU.add).then_inc(h_ready, 1)
                L.add(dve.tensor_tensor(eo[:, 2 * par + 1, :], eo[:, 2 * par + 1, :], G[:, 5, :], ALU.mult))

            def to_shared(t, j, par, L):
                L.add(dve.tensor_tensor(A[:, j, :], A[:, j, :], eo[:, 2 * par, :], ALU.add))
                L.wait(L.n)
                dve.tensor_tensor(A[:, j, :], A[:, j, :], eo[:, 2 * par + 1, :], ALU.add).then_inc(eo_used, 1)

            def task0(t):
                def body(j, par, weights):
                    L = Links(gate_link, 6 * (PAIRS * t + j))
                    if isinstance(j, int) and j == 0:
                        from_shared(t, j)
                    own_first(t, j, par, L)
                    own_second(t, j, par, L)
                    if isinstance(j, int) and j == 0:
                        weights()
                    to_shared(t, j, par, L)
                    if not (isinstance(j, int) and j == 0):
                        weights()
                    from_shared(t, j + 1)
                return body

            def task0_end(t):
                j, par = PAIRS - 1, 1

                def go():
                    L = Links(gate_link, 6 * (PAIRS * t + j))
                    gate_weights(t + 1, raw(graw1, t), K0)
                    for k in range(4):
                        x_tile(R, t, k)
                    own_first(t, j, par, L)
                    for k in range(4, KT - 1):
                        x_tile(R, t, k)
                    own_second(t, j, par, L)
                    x_tile(R, t, KT - 1)
                    to_shared(t, j, par, L)
                return go

            def task1(t, logits):
                def body(j, par, weights=lambda: None):
                    dve.wait_ge(g_loaded, 16 * (2 * t + 2))
                    dve.wait_ge(relu_done, UNITS * (2 * t + 2) + 2 * j + 2)
                    if logits:
                        wait_logits(t + 1, j)
                    dve.wait_ge(eo_used, PAIRS * (2 * t + 2) + j)
                    if not (isinstance(j, int) and j == 0):
                        dve.wait_ge(part_ready, PAIRS * t + j)
                    if not (isinstance(j, int) and j < 2):
                        dve.wait_ge(part_saved[par], 16 * (PAIRS // 2) * t + 8 * (j - par))
                    dve.tensor_tensor(sp[:, par, :], eo[:, 2 * par, :], G[:, 0, :], ALU.mult)
                    dve.tensor_tensor(tmp[:, :], eo[:, 2 * par + 1, :], G[:, 1, :], ALU.mult).then_inc(eo_used, 1)
                    dve.wait_ge(eo_used, PAIRS * (2 * t + 2) + j + 1)
                    dve.tensor_tensor(sp[:, par, :], sp[:, par, :], tmp[:, :], ALU.add).then_inc(part_ready, 1)
                    weights()
                return body

            def raw(g, t):
                return g[:, bass.ds(t * (KT * K0), KT * K0)]

            for c, n in ((0, 80), (1, 88)):
                dve.wait_ge(s_btr, c + 1)
                dve.tensor_copy(bias[:, c * 80:c * 80 + n], pu[:, 1, c * HALF:c * HALF + n]).then_inc(s_bias, 1)
            w_low(0, 0)
            for i in range(2 * KT):
                x_transposed(0, i)
            dve.wait_ge(s_graw, 16)
            gate_weights(0, graws[:, :], KS)
            dve.wait_ge(s_g0w, 16)
            dve.tensor_copy(g0w_sorted.rearrange("p (t c k) -> p t c k", t=T, c=K0),
                            g0w_raw.rearrange("p (t k c) -> p t c k", t=T, c=K0)).then_inc(g0w_sort, 1)
            dve.wait_ge(s_gb, 16 * 3)

            def shared0_end():
                for i in range(2 * KT):
                    x_transposed(1, i)
                shared0(PAIRS - 1, 1)

            one_pass("shared0", 0, 0, 0, KS, gb[:, 2 * T * K0:2 * T * K0 + KS], shared0, shared0_end,
                     lambda j, tiles: next_logits(0, gw_first, (eo_used, 0), j, tiles))

            def task(t, last):
                one_pass("task0", 2 * t + 1, None, t, K0, gb[:, bass.ds(t * K0, K0)], task0(t), task0_end(t))
                body = task1(t, not last)

                def task1_end():
                    if last:
                        for k in range(KT):
                            x_tile(A, T, k)
                    else:
                        for i in range(2 * KT):
                            x_transposed(t + 2, i)
                    body(PAIRS - 1, 1)

                one_pass("task1", 2 * t + 2, t + 1, t, K0, gb[:, bass.ds((T + t) * K0, K0)], body, task1_end,
                         None if last else
                         lambda j, tiles: next_logits(t + 1, gw_next, (part_ready, PAIRS * t), j, tiles))

            with dve.Fori(0, T - 1) as t:
                task(t, False)
            task(T - 1, True)

            w_low(LAST + 1, 1)

            def z_first(j, par, t):
                L = Links(z_link, 2 * (T * j + t))
                if t:
                    L.wait(L.n)
                elif isinstance(j, int) and j == 0:
                    dve.wait_ge(part_ready, PAIRS * T)
                else:
                    dve.wait_ge(z_raw, T * j)
                dve.wait_ge(relu_done, LAST + 2 * j + 1)
                dve.wait_ge(part_loaded[t], 16 * (j + 1))
                dve.wait_ge(g1_loaded[t], 16)
                L.wait(L.add(dve.tensor_tensor(tmp[:, :], eo[:, 2 * par, :], g1_tiles[t][:, 0, :], ALU.mult)))
                L.add(dve.tensor_tensor(part_tile[t], part_tile[t], tmp[:, :], ALU.add))

            def z_second(j, par, t):
                dve.wait_ge(relu_done, LAST + 2 * j + 2)
                if t:
                    dve.wait_ge(z_raw, T * j + t)
                else:
                    dve.wait_ge(z_link, 2 * T * (j + 1))
                dve.tensor_tensor(tmp[:, :], eo[:, 2 * par + 1, :], g1_tiles[t][:, 1, :], ALU.mult).then_inc(z_used, 1)
                dve.wait_ge(z_used, T * j + t + 1)
                dve.tensor_tensor(part_tile[t], part_tile[t], tmp[:, :], ALU.add).then_inc(z_raw, 1)

            def add_top(j, m):
                dve.wait_ge(steps_done, LAST + 6 * j + 2 + m + 1)
                if isinstance(j, int) and j == 0:
                    dve.wait_ge(xs_l, KT * (T + 1))
                    dve.tensor_copy(h1[:, m, :], pu[:, m % 2, :]).then_inc(top_added, 1)
                else:
                    dve.wait_ge(top_added, 4 * j + m - 3)
                    dve.tensor_tensor(h1[:, m, :], pu[:, m % 2, :], h1[:, m, :], ALU.add).then_inc(top_added, 1)

            def split_z(j):
                last = isinstance(j, int) and j == PAIRS - 1
                zh_, zl_ = (xh, xl) if last else (zh, zl)
                for t in range(T):
                    dve.wait_ge(z_h, T * j + t + 1)
                    low(zl_[:, t, :], part_tile[t], zh_[:, t, :], z_l)

            rows = dict(k=slice(0, DC), cols=slice(0, WM))
            dve.wait_ge(dense_h, 1)
            low(zl[0:DC, 0, :].rearrange("p (h c) -> p h c", h=2), pm[0:DC, 0:2, :],
                zh[0:DC, 0, :].rearrange("p (h c) -> p h c", h=2), dense_l)
            w_low(LAST + 2, 0, **rows)
            for t in range(T - 1):
                z_first(0, 0, t)
            w_low(LAST + 3, 1, **rows)
            add_top(0, 0)
            add_top(0, 1)
            w_low(LAST + 4, 0)
            add_top(0, 2)
            add_top(0, 3)
            z_first(0, 0, T - 1)
            z_second(0, 0, 0)
            w_low(LAST + 5, 1)
            for t in range(1, T):
                z_second(0, 0, t)
            split_z(0)

            def last_pair(j, par):
                n = LAST + 4 * j
                last = isinstance(j, int) and j == PAIRS - 1
                w_low(n + 2, 0)
                for t in range(T):
                    z_first(j, par, t)
                w_low(n + 3, 1)
                if isinstance(j, int) and j == 1:
                    add_top(j, 0)
                    z_second(j, par, 0)
                    add_top(j, 1)
                    z_second(j, par, 1)
                    w_low(n + 4, 0)
                    add_top(j, 2)
                    z_second(j, par, 2)
                    z_second(j, par, 3)
                else:
                    z_second(j, par, 0)
                    add_top(j, 0)
                    z_second(j, par, 1)
                    z_second(j, par, 2)
                    add_top(j, 1)
                    w_low(n + 4, 0)
                    z_second(j, par, 3)
                    if last:
                        split_z(j)
                    add_top(j, 2)
                add_top(j, 3)
                w_low(n + 5, 1)
                if not last:
                    split_z(j)

            pairs(dve, last_pair)
            for m in range(M1):
                dve.wait_ge(steps_done, LAST + 6 * PAIRS + m + 1)
                dve.wait_ge(top_added, 4 * (PAIRS - 1) + m + 1)
                dve.tensor_tensor(h1[:, m, :], pu[:, m % 2, :], h1[:, m, :], ALU.add).then_inc(top_added, 1)
                if m == 1:
                    w_low(LAST + 4 * PAIRS + 2, 0)
                dve.wait_ge(top_added, 4 * PAIRS + m + 1)
                dve.tensor_scalar(eo[:, m, :], h1[:, m, :], bias[:, 160 + m:161 + m], 0.0, ALU.add,
                                  ALU.max).then_inc(h1_relu, 1)
                dve.wait_ge(h1_relu, m + 1)
                dve.wait_ge(h1_h, m + 1)
                low(zl[:, m, :], eo[:, m, :], zh[:, m, :], h1_l)


_TABLES = ['tbl_0', 'tbl_1', 'tbl_2', 'tbl_3', 'tbl_4']
_FIRST = ['dense_ctx', 'ids']
_REST = ['W_top1', 'b_top1', 'W_top2', 'b_top2', 'W_top3', 'L0_rec_W0', 'L0_rec_b0', 'L0_rec_G0w', 'L0_rec_G0b',
         'L0_rec_Gs0w', 'L0_rec_Gs0b', 'L0_rec_W1', 'L0_rec_b1', 'L0_rec_G1w', 'L0_rec_G1b']


def kernel(**inputs):
    import numpy as _np
    import concourse.bacc as _bacc
    from concourse import mybir as _mybir
    from concourse.bass_utils import run_bass_kernel_spmd as _run

    nc = _bacc.Bacc("TRN2", target_bir_lowering=False, num_devices=1)
    arrays, args = {}, {}
    for name in _FIRST + _TABLES + _REST:
        a = _np.ascontiguousarray(inputs[name])
        arrays[f"in_{name}"] = a
        args[name] = nc.dram_tensor(f"in_{name}", a.shape, _mybir.dt.from_np(a.dtype), kind="ExternalInput").ap()
    y = nc.dram_tensor("y", (1024, 1), _mybir.dt.float32, kind="ExternalOutput").ap()
    dlrm_tower(nc, *[args[n] for n in _FIRST], [args[n] for n in _TABLES], *[args[n] for n in _REST], y)
    r = _run(nc, [arrays], core_ids=[0])
    return r.results[0]["y"]
```
